# Optimizing a Trainium2 kernel written in Bass

```python
import numpy as np
import jax
import jax.numpy as jnp

def _softmax(x, axis=-1):
    return jax.nn.softmax(x, axis=axis)
def _gelu(x):
    return jax.nn.gelu(x, approximate=True)
def _silu(x):
    return jax.nn.silu(x)
def _sigmoid(x):
    return jax.nn.sigmoid(x)
def _layernorm(x, axis=-1, eps=1e-5):
    m = jnp.mean(x, axis=axis, keepdims=True)
    v = jnp.var(x, axis=axis, keepdims=True)
    return (x - m) / jnp.sqrt(v + eps)
def _scatter_add(tgt, idx, src, axis=0):
    return tgt.at[idx].add(src)
def _segment_sum(src, seg, n):
    return jax.ops.segment_sum(src, seg, n)

kernel_name = 'mk_adj_resnorm_d2_adj_128_eccdae'

def setup_inputs(seed: int = 0):
    np.random.seed(seed)
    _w = jnp.asarray
    def _rec_inputs():
        import jax
        import jax.numpy as jnp
        _gk = jax.random.key(seed)
        x = -0.0005207 + 1.001 * jax.random.normal(jax.random.fold_in(_gk, 1), (2708, 128), jnp.float32)
        _a = jax.random.bernoulli(jax.random.fold_in(_gk, 2), 0.00590842, (2708, 2708))
        _a = jnp.logical_or(_a, jnp.swapaxes(_a, -1, -2))
        _a = jnp.logical_or(_a, jnp.eye(2708, dtype=bool))
        _af = _a.astype(jnp.float32)
        adj = _af
        return x, adj
    x, adj = _rec_inputs()
    def _L0_gnn_setup():
        import jax, jax.numpy as jnp
        import numpy as np
        N = 16384
        U = 128
        AVG_DEGREE = 32
        key = jax.random.key(seed)
        kx, ka, kw = jax.random.split(key, 3)
        x = jax.random.normal(kx, (N, U), dtype=jnp.float32)
        adj = (jax.random.uniform(ka, (N, N)) < AVG_DEGREE / N).astype(jnp.float32)
        W = jax.random.normal(kw, (U, U), dtype=jnp.float32) * 0.05
        b = jnp.zeros((U,), dtype=jnp.float32)
        return {'x': x, 'adj': adj, 'W': W, 'b': b}
    _L0_gnn_all = _L0_gnn_setup()
    _L0_gnn_in = {k: v for k, v in _L0_gnn_all.items() if k in ('W', 'b', )}
    del _L0_gnn_all

    def _L1_gnn_setup():
        import jax, jax.numpy as jnp
        import numpy as np
        N = 1024
        D = 128
        H = 8
        key = jax.random.key(seed)
        ks = jax.random.split(key, 7)
        s = (D * H) ** (-0.5)
        return {'x': jax.random.normal(ks[0], (N, D), dtype=jnp.float32), 'spatial_encoding': jax.random.normal(ks[1], (N, N), dtype=jnp.float32), 'edge_encoding': jax.random.normal(ks[2], (N, N), dtype=jnp.float32), 'Wq': jax.random.normal(ks[3], (D * H, D), dtype=jnp.float32) * s, 'Wk': jax.random.normal(ks[4], (D * H, D), dtype=jnp.float32) * s, 'Wv': jax.random.normal(ks[5], (D * H, D), dtype=jnp.float32) * s, 'Wo': jax.random.normal(ks[6], (D, D * H), dtype=jnp.float32) * s}
    _L1_gnn_all = _L1_gnn_setup()
    _L1_gnn_in = {k: v for k, v in _L1_gnn_all.items() if k in ('Wq', 'Wk', 'Wv', 'Wo', )}
    del _L1_gnn_all

    return {
        "x": x,
        "adj": adj,
        "L0_gnn_W": _L0_gnn_in["W"],
        "L0_gnn_b": _L0_gnn_in["b"],
        "L1_gnn_Wq": _L1_gnn_in["Wq"],
        "L1_gnn_Wk": _L1_gnn_in["Wk"],
        "L1_gnn_Wv": _L1_gnn_in["Wv"],
        "L1_gnn_Wo": _L1_gnn_in["Wo"],
    }

def reference(x, adj, L0_gnn_W, L0_gnn_b, L1_gnn_Wq, L1_gnn_Wk, L1_gnn_Wv, L1_gnn_Wo):
    import jax
    import jax.numpy as jnp
    def _L0_gnn_ref(x, adj, W, b):
        import jax, jax.numpy as jnp
        import numpy as np
        N = 16384
        U = 128
        AVG_DEGREE = 32
        adj = jax.lax.stop_gradient(adj)
        neigh1 = adj @ x
        x1 = jax.nn.swish(neigh1 @ W + b)
        neigh2 = adj @ x1
        x2 = jax.nn.swish(neigh2 @ W + b)
        return x2

    def _L1_gnn_ref(x, spatial_encoding, edge_encoding, Wq, Wk, Wv, Wo):
        import jax, jax.numpy as jnp
        import numpy as np
        N = 1024
        D = 128
        H = 8
        n, d = x.shape
        h = Wq.shape[0] // d
        scale = d ** (-0.5)
        q = (x @ Wq.T).reshape(d, n, h)
        k = (x @ Wk.T).reshape(d, n, h)
        v = (x @ Wv.T).reshape(d, n, h)
        a = jnp.einsum('dnh,dmh->dnm', q, k) * scale
        a = a + spatial_encoding + edge_encoding
        a = jax.nn.softmax(a, axis=2)
        out = jnp.einsum('dnm,dmh->dnh', a, v)
        out = out.reshape(n, h * d)
        return out @ Wo.T

    x = _layernorm(x + _L0_gnn_ref(x, adj, L0_gnn_W, L0_gnn_b), axis=-1)
    x = _layernorm(x + _L1_gnn_ref(x, adj, adj, L1_gnn_Wq, L1_gnn_Wk, L1_gnn_Wv, L1_gnn_Wo), axis=-1)
    return x


_drawn_inputs = setup_inputs


def setup_inputs(seed=0):
    import zlib

    import numpy as np

    out = dict(_drawn_inputs(seed))
    spreads = {'L0_gnn_b': (0.0, 0.1)}
    factors = {'L1_gnn_Wq': 8.0, 'L1_gnn_Wk': 8.0}
    for name, (base, spread) in spreads.items():
        noise = np.random.default_rng([zlib.crc32(name.encode()), seed]).standard_normal(out[name].shape)
        drawn = base * np.exp(spread * noise) if base else spread * noise
        out[name] = jnp.asarray(drawn.astype(out[name].dtype))
    for name, factor in factors.items():
        out[name] = (out[name] * factor).astype(out[name].dtype)
    return out
```

```python
from contextlib import ExitStack

import concourse.bass as bass
from concourse import mybir

F32 = mybir.dt.float32
BF16 = mybir.dt.bfloat16
I32 = mybir.dt.int32
ALU = mybir.AluOpType
ACT = mybir.ActivationFunctionType
AX = mybir.AxisListType

N = 2708
D = 128
H = 8
T = 22
FULL = N // T
REST = N - FULL * T
PR = FULL + 1
CH = 452
HALF = 3 * CH
NP = 2 * HALF
QT = HALF // 4
CW = H * D
G = N * D
PAIRS = T // 2
STEPS = 2 * PAIRS
NB = -(-N // 128)
TERMS = 6 * H
ROWS = TERMS + 2
SCALE = float(D) ** -0.5
EPS = 1e-5
ADJ_GAIN = 2.0
HEADS = D
BY_DVE, BY_POOL = (0, 1), 2
LEAST = 2.0 ** -64
QK_HALF = 3 * PAIRS


def chunk(keep, r, half, t, c):
    i = 3 * (t % 2) + c
    if i < 4:
        return keep["adj_a"][0:r, half, t // 2, i * CH:(i + 1) * CH]
    return keep["adj_b"][0:r, half, t // 2, (i - 4) * CH:(i - 3) * CH]


def rows(t):
    return PR if t < REST else FULL


def layer0(nc, dram, keep):
    x, adjT, W, b = dram["x"], dram["adjT"], dram["W"], dram["b"]
    adj_a, adj_b, yT, ident = keep["adj_a"], keep["adj_b"], keep["yT"], keep["ident"]
    with ExitStack() as ctx:
        def sb(name, shape, dt=F32):
            return ctx.enter_context(nc.sbuf_tensor(name, shape, dt))

        def sem(name):
            return ctx.enter_context(nc.semaphore(name))

        xs = sb("xs", [PR, T, D])
        part = [sb(f"part{k}", [PR, T, D], BF16) for k in range(3)]
        x1 = keep["spare"][0:PR, 0:T * D].rearrange("p (t d) -> p t d", d=D)
        nT = yT
        w_sb = sb("w_sb", [D, D])
        b_sb = sb("b_sb", [1, D])
        ones_row = sb("ones_row", [1, 128])
        tmp = keep["spare"][0:PR, T * D:(T + 4) * D].rearrange("p (t d) -> p t d", d=D)
        stats = sb("stats", [PR, T, 6])
        mv = sb("mv", [PR, T, 2])
        rstd = sb("rstd", [PR, T])
        ps = ctx.enter_context(nc.psum_tensor("ps0", [128, 8, 512], F32))

        id_made = sem("id_made")
        pads = sem("pads")
        x_in = sem("x_in")
        w_in = sem("w_in")
        adj_in = [sem(f"adj_in{t}") for t in range(T)]
        split_vec = sem("split_vec")
        split_act = sem("split_act")
        summed = sem("summed")
        copied_v = sem("copied_v")
        copied_a = sem("copied_a")
        lin = sem("lin")
        clamped = sem("clamped")
        expd = sem("expd")
        chain = sem("chain")
        swished = sem("swished")
        varred = sem("varred")
        rooted = sem("rooted")
        normed = sem("normed")
        turned = sem("turned")
        placed = sem("placed")
        y_out = sem("y_out")
        GROUPS = [(g, min(4, T - g)) for g in range(0, T, 4)]
        block = ctx.enter_context(nc.Block())

        @block.sync
        def _(sp):
            sp.dma_start(w_sb[:], W).then_inc(w_in, 16)
            sp.dma_start(b_sb[:], b.rearrange("(a d) -> a d", a=1)).then_inc(w_in, 16)
            sp.wait_ge(pads, 1)
            sp.dma_start(xs[0:FULL], x[0:FULL * T].rearrange("(p t) d -> p t d", t=T)).then_inc(x_in, 16)
            sp.dma_start(xs[FULL:PR, 0:REST], x[FULL * T:N].rearrange("(p t) d -> p t d", t=REST)).then_inc(x_in, 16)
            sp.wait_ge(normed, T)
            y1 = dram["y1"]
            sp.dma_start(y1[0:FULL * T].rearrange("(p t) d -> p t d", t=T), xs[0:FULL]).then_inc(y_out, 16)
            sp.dma_start(y1[FULL * T:N].rearrange("(p t) d -> p t d", t=REST), xs[FULL:PR, 0:REST]).then_inc(y_out, 16)
            sp.wait_ge(y_out, 32)

        @block.gpsimd
        def _(pool):
            nc.gpsimd.memset(ident[:], 0.0).then_inc(id_made, 1)
            pool.wait_ge(id_made, 1)
            nc.gpsimd.affine_select(out=ident[:], in_=ident[:], compare_op=ALU.not_equal, fill=1.0, base=0,
                                    pattern=[[-1, 128]], channel_multiplier=1).then_inc(id_made, 1)
            whole = adjT[0:FULL * T].rearrange("(p t) n -> p t n", t=T)
            for t in range(T):
                for half in range(2):
                    n0, n1 = half * HALF, min(N, (half + 1) * HALF)
                    if t % 2 == 0:
                        pieces = [(adj_a, 0, n0, n1)]
                    else:
                        pieces = [(adj_a, 3 * CH, n0, n0 + CH), (adj_b, 0, n0 + CH, n1)]
                    for to, at, lo, hi in pieces:
                        pool.dma_start(to[0:FULL, half, t // 2, at:at + hi - lo], whole[:, t, lo:hi]).then_inc(adj_in[t], 16)
                        if t < REST:
                            pool.dma_start(to[FULL:PR, half, t // 2, at:at + hi - lo],
                                           adjT[FULL * T + t:FULL * T + t + 1, lo:hi]).then_inc(adj_in[t], 16)

        def aggregate(pe, first):
            for t in range(T):
                if first:
                    pe.wait_ge(adj_in[t], 32 * (1 + t % 2) * (2 if t < REST else 1))
                for k in range(3):
                    for c in range(6):
                        last = nc.tensor.matmul(ps[:, c, 0:CH], part[k][0:rows(t), t, :],
                                                chunk(keep, rows(t), c // 3, t, c % 3),
                                                start=(t == 0 and k == 0), stop=(t == T - 1 and k == 2))
            last.then_inc(summed, 1)

        def linear(pe, rnd):
            pe.wait_ge(copied_v, 3 * (rnd + 1))
            pe.wait_ge(copied_a, 3 * (rnd + 1))
            for i, (g, n) in enumerate(GROUPS):
                if i >= 2 or rnd:
                    pe.wait_ge(swished, rnd * len(GROUPS) + i - 1)
                for j in range(n):
                    nc.tensor.matmul(ps[0:PR, 6 + i % 2, j * D:(j + 1) * D],
                                     nT[:, g + j:g + j + T * (PR - 1) + 1:T], w_sb[:], start=True, stop=False)
                    last = nc.tensor.matmul(ps[0:PR, 6 + i % 2, j * D:(j + 1) * D], ones_row[0:1, 0:PR], b_sb[:],
                                            start=False, stop=True)
                last.then_inc(lin, 1)

        @block.tensor
        def _(pe):
            pe.wait_ge(split_act, 2)
            pe.wait_ge(split_vec, 2)
            aggregate(pe, True)
            pe.wait_ge(w_in, 32)
            pe.wait_ge(pads, 2)
            linear(pe, 0)
            pe.wait_ge(split_act, 4)
            pe.wait_ge(split_vec, 4)
            aggregate(pe, False)
            linear(pe, 1)
            pe.wait_ge(id_made, 2)
            for i, (g, n) in enumerate(GROUPS):
                pe.wait_ge(normed, g + n)
                if i >= 2:
                    pe.wait_ge(placed, i - 1)
                for j in range(n):
                    last = nc.tensor.transpose(ps[:, 4 + i % 2, j * D:j * D + PR], xs[0:PR, g + j, :], ident[0:PR, 0:PR])
                last.then_inc(turned, 1)

        @block.scalar
        def _(act):
            act.wait_ge(x_in, 32)
            for rnd in range(2):
                if rnd:
                    act.wait_ge(swished, len(GROUPS))
                    act.wait_ge(summed, 1)
                nc.scalar.copy(part[0][:], xs[:] if rnd == 0 else x1).then_inc(split_act, 1)
                act.wait_ge(split_vec, 2 * rnd + 1)
                nc.scalar.copy(part[1][:], x1).then_inc(split_act, 1)
                act.wait_ge(summed, rnd + 1)
                for c in range(3):
                    w = min(CH, N - c * CH)
                    nc.scalar.copy(nT[:, c * CH:c * CH + w], ps[:, c, 0:w]).then_inc(copied_a, 1)
                for i, (g, n) in enumerate(GROUPS):
                    act.wait_ge(clamped, rnd * len(GROUPS) + i + 1)
                    nc.scalar.activation(tmp[:, 0:n], tmp[:, 0:n], ACT.Exp, scale=-1.0).then_inc(expd, 1)
            act.wait_ge(varred, 1)
            nc.scalar.activation(rstd[:], rstd[:], ACT.Sqrt).then_inc(rooted, 1)

        @block.vector
        def _(dve):
            links = [0]

            def link(ins):
                links[0] += 1
                ins.then_inc(chain, 1)
                dve.wait_ge(chain, links[0])

            nc.vector.memset(xs[:], 0.0).then_inc(pads, 1)
            link(nc.vector.memset(nT[:, N:], 0.0))
            link(nc.vector.memset(adj_a[:, 1, :, 3 * CH - (NP - N):3 * CH], 0.0))
            link(nc.vector.memset(adj_b[:, 1, :, 2 * CH - (NP - N):2 * CH], 0.0))
            nc.vector.memset(ones_row[:], 1.0).then_inc(pads, 1)
            dve.wait_ge(x_in, 32)
            for rnd in range(2):
                src = xs[:] if rnd == 0 else x1
                dve.wait_ge(split_act, 2 * rnd + 1)
                nc.vector.tensor_tensor(x1, src, part[0][:], ALU.subtract).then_inc(split_vec, 1)
                dve.wait_ge(split_vec, 2 * rnd + 1)
                dve.wait_ge(split_act, 2 * rnd + 2)
                if rnd:
                    dve.wait_ge(summed, 1)
                nc.vector.tensor_tensor(part[2][:], x1, part[1][:], ALU.subtract).then_inc(split_vec, 1)
                dve.wait_ge(summed, rnd + 1)
                for c in range(3, 6):
                    w = min(CH, N - c * CH)
                    nc.vector.tensor_copy(nT[:, c * CH:c * CH + w], ps[:, c, 0:w]).then_inc(copied_v, 1)
                if rnd == 0:
                    dve.wait_ge(split_vec, 2)
                for i, (g, n) in enumerate(GROUPS):
                    dve.wait_ge(lin, rnd * len(GROUPS) + i + 1)
                    z = ps[0:PR, 6 + i % 2, 0:n * D].rearrange("p (j d) -> p j d", d=D)
                    nc.vector.tensor_scalar(tmp[:, 0:n], z, -80.0, None, ALU.max).then_inc(clamped, 1)
                    dve.wait_ge(expd, rnd * len(GROUPS) + i + 1)
                    link(nc.vector.tensor_scalar(tmp[:, 0:n], tmp[:, 0:n], 1.0, None, ALU.add))
                    link(nc.vector.reciprocal(tmp[:, 0:n], tmp[:, 0:n]))
                    nc.vector.tensor_tensor(x1[:, g:g + n], z, tmp[:, 0:n], ALU.mult).then_inc(swished, 1)
                    dve.wait_ge(swished, rnd * len(GROUPS) + i + 1)
            link(nc.vector.tensor_tensor(xs[:], xs[:], x1, ALU.add))
            for t in range(T):
                last = nc.vector.bn_stats(stats[:, t], xs[:, t])
            link(last)
            for t in range(T):
                last = nc.vector.bn_aggr(mv[:, t], stats[:, t])
            link(last)
            nc.vector.tensor_scalar(rstd[:], mv[:, :, 1], EPS, None, ALU.add).then_inc(varred, 1)
            dve.wait_ge(rooted, 1)
            link(nc.vector.reciprocal(rstd[:], rstd[:]))
            for t in range(T):
                nc.vector.tensor_scalar(xs[:, t], xs[:, t], mv[:, t, 0:1], rstd[:, t:t + 1],
                                        ALU.subtract, ALU.mult).then_inc(normed, 1)
            yT_tiles = yT[:].rearrange("d (p t) -> d t p", t=T)
            for i, (g, n) in enumerate(GROUPS):
                dve.wait_ge(turned, i + 1)
                nc.vector.tensor_copy(yT_tiles[:, g:g + n, 0:PR],
                                      ps[:, 4 + i % 2, 0:n * D].rearrange("p (j d) -> p j d", d=D)[:, :, 0:PR]).then_inc(placed, 1)
            dve.wait_ge(placed, len(GROUPS))


def project(nc, dram, keep):
    yT = keep["yT"]
    with ExitStack() as ctx:
        def sb(name, shape, dt=F32):
            return ctx.enter_context(nc.sbuf_tensor(name, shape, dt))

        def sem(name):
            return ctx.enter_context(nc.semaphore(name))

        w = {c: sb(f"w{c}", [D, CW]) for c in "kqv"}
        parts = sb("parts", [128, 2, 26, D], BF16)
        rem = keep["spare"][:, 0 * CW:2 * CW].rearrange("p (a c) -> p a c", c=CW)
        sq = keep["spare"][:, 2 * CW:4 * CW].rearrange("p (a c) -> p a c", c=CW)
        v_sb = keep["spare"][:, 4 * CW:6 * CW].rearrange("p (a c) -> p a c", c=CW)
        nsq = sb("nsq", [128, 2, D])
        kmax = sb("kmax", [128, NB])
        kall = sb("kall", [128, 2])
        ps = ctx.enter_context(nc.psum_tensor("ps1", [128, 8, 512], F32))

        w_in = [sem(f"w_in_{c}") for c in "kqv"]
        proj = sem("proj")
        projv = sem("projv")
        high = sem("high")
        remd = sem("remd")
        mid = sem("mid")
        low = sem("low")
        sqd = sem("sqd")
        nsqd = sem("nsqd")
        maxd = sem("maxd")
        allmax = sem("allmax")
        rooted = sem("rooted")
        guard_steps = sem("guard_steps")
        guarded = sem("guarded")
        v_cp = sem("v_cp")
        stored = [sem(f"stored{j}") for j in range(2)]
        v_out = [sem(f"v_out{j}") for j in range(2)]
        chain = sem("chain_p")
        block = ctx.enter_context(nc.Block())
        size = [min(128, N - 128 * b) for b in range(NB)]
        jobs = [("k", b) for b in range(NB)] + [("q", b) for b in range(NB)]

        @block.sync
        def _(sp):
            for c, s in zip("kqv", w_in):
                sp.dma_start(w[c][:], dram["w" + c]).then_inc(s, 16)
            for i, (c, b) in enumerate(jobs):
                sp.wait_ge(low, i + 1)
                sp.wait_ge(mid, i + 1)
                n = 24
                if c == "q":
                    sp.wait_ge(guarded, b + 1)
                    n = 26
                dst = dram[c + "d"][0:n, 128 * 128 * b:128 * 128 * b + 128 * size[b]].rearrange("r (i c) -> i r c", c=D)
                sp.dma_start(dst, parts[0:size[b], i % 2, 0:n]).then_inc(stored[i % 2], 16)
                if c == "q":
                    sp.wait_ge(v_cp, b + 1)
                    sp.dma_start(dram["vd"][128 * b:128 * b + size[b]], v_sb[0:size[b], b % 2]).then_inc(v_out[b % 2], 16)
            for j in range(2):
                sp.wait_ge(stored[j], 16 * NB)
                sp.wait_ge(v_out[j], 16 * (NB // 2))

        @block.tensor
        def _(pe):
            def go(c, b, bank):
                for j in range(2):
                    last = nc.tensor.matmul(ps[0:size[b], bank + j, :], yT[:, 128 * b:128 * b + size[b]],
                                            w[c][:, 512 * j:512 * (j + 1)], start=True, stop=True)
                return last

            for i, (c, b) in enumerate(jobs):
                if b == 0:
                    pe.wait_ge(w_in["kqv".index(c)], 16)
                if i >= 2:
                    pe.wait_ge(remd, i - 1)
                    pe.wait_ge(sqd, i - 1)
                go(c, b, 2 * (i % 2)).then_inc(proj, 1)
                if c == "q":
                    if b == 0:
                        pe.wait_ge(w_in[2], 16)
                    if b >= 2:
                        pe.wait_ge(v_cp, b - 1)
                    go("v", b, 4 + 2 * (b % 2)).then_inc(projv, 1)

        def bank(i, n):
            return ps[0:n, 2 * (i % 2):2 * (i % 2) + 2, :].rearrange("p a b -> p (a b)")

        @block.scalar
        def _(act):
            for i, (c, b) in enumerate(jobs):
                n, sc = size[b], SCALE if c == "q" else 1.0
                act.wait_ge(proj, i + 1)
                if i >= 2:
                    act.wait_ge(stored[i % 2], 16 * (i // 2))
                nc.scalar.activation(parts[0:n, i % 2, 0:8].rearrange("p a b -> p (a b)"), bank(i, n),
                                     ACT.Copy, scale=sc).then_inc(high, 1)
                if i >= 2:
                    act.wait_ge(nsqd, i - 1)
                nc.scalar.activation(sq[0:n, i % 2], bank(i, n), ACT.Square, scale=sc).then_inc(sqd, 1)
                act.wait_ge(remd, i + 1)
                nc.scalar.copy(parts[0:n, i % 2, 8:16].rearrange("p a b -> p (a b)"), rem[0:n, i % 2]).then_inc(mid, 1)
                if c == "q":
                    act.wait_ge(allmax, 1)
                    act.wait_ge(nsqd, i + 1)
                    nc.scalar.activation(nsq[0:n, i % 2], nsq[0:n, i % 2], ACT.Sqrt, scale=kall[0:n, 1:2]).then_inc(rooted, 1)

        @block.vector
        def _(dve):
            nc.vector.memset(kmax[:], 0.0).then_inc(chain, 1)
            dve.wait_ge(chain, 1)
            for i, (c, b) in enumerate(jobs):
                n, sc = size[b], SCALE if c == "q" else 1.0
                dve.wait_ge(sqd, i + 1)
                if i >= 2:
                    dve.wait_ge(mid, i - 1)
                    dve.wait_ge(low, i - 1)
                nc.vector.scalar_tensor_tensor(out=rem[0:n, i % 2], in0=bank(i, n), scalar=sc,
                                               in1=parts[0:n, i % 2, 0:8].rearrange("p a b -> p (a b)"),
                                               op0=ALU.mult, op1=ALU.subtract).then_inc(remd, 1)
                if c == "q":
                    dve.wait_ge(projv, b + 1)
                    if b >= 2:
                        dve.wait_ge(v_out[b % 2], 16 * (b // 2))
                    nc.vector.tensor_copy(v_sb[0:n, b % 2],
                                          ps[0:n, 4 + 2 * (b % 2):6 + 2 * (b % 2), :].rearrange("p a b -> p (a b)")).then_inc(v_cp, 1)
                if i >= 2 and c == "q" and b >= 2:
                    dve.wait_ge(guarded, b - 1)
                nc.vector.tensor_reduce(nsq[0:n, i % 2], sq[0:n, i % 2].rearrange("p (h c) -> p c h", h=H),
                                        AX.X, ALU.add).then_inc(nsqd, 1)
                dve.wait_ge(nsqd, i + 1)
                if c == "k":
                    nc.vector.tensor_reduce(kmax[0:n, b:b + 1], nsq[0:n, i % 2], AX.X, ALU.max).then_inc(maxd, 1)
                    if b == NB - 1:
                        dve.wait_ge(maxd, NB)
                        nc.vector.tensor_reduce(kall[:, 0:1], kmax[:], AX.X, ALU.max).then_inc(maxd, 1)
                dve.wait_ge(mid, i + 1)
                dve.wait_ge(remd, i + 1)
                nc.vector.tensor_tensor(parts[0:n, i % 2, 16:24].rearrange("p a b -> p (a b)"), rem[0:n, i % 2],
                                        parts[0:n, i % 2, 8:16].rearrange("p a b -> p (a b)"),
                                        ALU.subtract).then_inc(low, 1)
                if c == "q":
                    dve.wait_ge(rooted, b + 1)
                    nc.vector.tensor_scalar(nsq[0:n, i % 2], nsq[0:n, i % 2], -1.0, -ADJ_GAIN,
                                            ALU.mult, ALU.add).then_inc(guard_steps, 1)
                    dve.wait_ge(guard_steps, 2 * b + 1)
                    nc.vector.tensor_copy(parts[0:n, i % 2, 24], nsq[0:n, i % 2]).then_inc(guard_steps, 1)
                    dve.wait_ge(guard_steps, 2 * b + 2)
                    nc.vector.tensor_tensor(parts[0:n, i % 2, 25], nsq[0:n, i % 2], parts[0:n, i % 2, 24],
                                            ALU.subtract).then_inc(guarded, 1)

        @block.gpsimd
        def _(pool):
            pool.wait_ge(maxd, NB + 1)
            nc.gpsimd.partition_all_reduce(kall[:, 1:2], kall[:, 0:1], 128, bass.bass_isa.ReduceOp.max).then_inc(allmax, 1)


class Always:

    def __enter__(self):
        return self

    def __exit__(self, *_):
        return False


def when(eng, flag):
    if flag is None:
        return Always()
    return eng.If(eng.value_load(flag[0:1, 0:1], min_val=0, max_val=1) != 0)


def weigh(nc, keep):
    adj_b = keep["adj_b"].rearrange("p h a n -> p (h a) n")
    weight = keep["weight"][:].rearrange("p h a n -> p (h a) n")
    n = 2 * PAIRS
    with ExitStack() as ctx:
        last_row = ctx.enter_context(nc.sbuf_tensor("last_row", [PR, 2 * CH], BF16))
        done = ctx.enter_context(nc.semaphore("weights_done"))
        block = ctx.enter_context(nc.Block())

        @block.scalar
        def _(act):
            nc.scalar.copy(last_row[0:FULL], adj_b[0:FULL, n - 1]).then_inc(done, 1)
            act.wait_ge(done, 1)
            steps, lo = 1, 0
            while lo < n - 1:
                hi = min((n + lo) // 2, n - 1)
                cuts = sorted({lo, hi} | {c for c in (1, PAIRS, PAIRS + 1) if lo < c < hi})
                for c0, c1 in zip(cuts, cuts[1:]):
                    r = PR if c0 % PAIRS == 0 else FULL
                    nc.scalar.activation(weight[0:r, c0:c1], adj_b[0:r, c0:c1], ACT.Exp, scale=ADJ_GAIN).then_inc(done, 1)
                    steps += 1
                    act.wait_ge(done, steps)
                lo = hi
            nc.scalar.activation(weight[0:FULL, n - 1], last_row[0:FULL], ACT.Exp, scale=ADJ_GAIN).then_inc(done, 1)
            act.wait_ge(done, steps + 1)


def attend(nc, dram, keep, tag, flag=None):
    adj_a, weight = keep["adj_a"], keep["weight"]
    with ExitStack() as ctx:
        def sb(name, shape, dt=F32):
            return ctx.enter_context(nc.sbuf_tensor(name + tag, shape, dt))

        def sem(name):
            return ctx.enter_context(nc.semaphore(name + tag))

        prob = sb("prob", [PR, 2, NP])
        q_st = sb("q_st", [128, 2, HALF], BF16)
        k_st = sb("k_st", [128, 2, N], BF16)
        v_in_sb = sb("v_in_sb", [PR, 2, T * H])
        v_aug = sb("v_aug", [PR, 2, T, 32])
        o_sb = sb("o_sb", [128, 2, QT])
        one = sb("one", [PR, T * H])
        S = ctx.enter_context(nc.psum_tensor("scores" + tag, [128, 6, 512], F32))
        O = ctx.enter_context(nc.psum_tensor("sums" + tag, [128, 2, 512], F32))

        ready = sem("ready")
        q_in = [sem(f"q_in{j}") for j in range(2)]
        k_in = [sem(f"k_in{j}") for j in range(2)]
        v_in = [sem(f"v_in{j}") for j in range(2)]
        qk = sem("qk")
        added = sem("added")
        exps = sem("exps")
        pv = sem("pv")
        weighed = sem("weighed")
        v_placed = sem("v_placed")
        o_copied = sem("o_copied")
        stores = sem("stores")
        o_out = [sem(f"o_out{j}") for j in range(2)]
        QK0 = 2 * QK_HALF + 1
        PV0 = 2 * T - 3 + 1
        block = ctx.enter_context(nc.Block())

        def halves_multiplied(eng, n):
            eng.wait_ge(qk, n * QK_HALF + 1)

        def halves_summed(eng, n):
            eng.wait_ge(pv, n * T + 1)

        qd = dram["qd"]
        kd = dram["kd"]
        vflat = dram["vd"].rearrange("i c -> (i c)")

        @block.sync
        def _(sp):
            with when(sp, flag):
                for half in range(2):
                    sp.sem_inc(o_out[half], 16)

                def load_k(at, par):
                    for r0, n in ((0, 24), (24, 16), (40, 8)):
                        sp.dma_start(k_st[r0:r0 + n, par], kd[0:n, bass.ds(at, N)]).then_inc(k_in[par], 16)

                def load_q(at, half):
                    w = min(HALF, N - half * HALF)
                    cols = bass.ds(at, w)
                    for j in range(3):
                        sp.dma_start(q_st[8 * j:8 * j + 8, half, 0:w], qd[0:8, cols]).then_inc(q_in[half], 16)
                    for j in range(2):
                        sp.dma_start(q_st[24 + 8 * j:32 + 8 * j, half, 0:w], qd[8:16, cols]).then_inc(q_in[half], 16)
                    sp.dma_start(q_st[40:ROWS, half, 0:w], qd[16:26, cols]).then_inc(q_in[half], 16)

                def load_v(at, rest, par):
                    sp.dma_start(v_in_sb[0:FULL, par], vflat[bass.ds(at, FULL * T * H)].rearrange("(p c) -> p c", c=T * H))\
                      .then_inc(v_in[par], 16)
                    sp.dma_start(v_in_sb[FULL:PR, par, 0:REST * H],
                                 vflat[bass.ds(rest, REST * H)].rearrange("(p c) -> p c", p=1)).then_inc(v_in[par], 16)

                def store(at, half):
                    for j in range(4):
                        w = min(QT, N - half * HALF - j * QT)
                        sp.dma_start(dram["od"][0:H + 1, bass.ds(at[j], w)],
                                     o_sb[32 * j:32 * j + H + 1, half, 0:w]).then_inc(o_out[half], 16)

                sp.wait_ge(ready, 2)
                with sp.Fori(0, HEADS // 2) as i:
                    for par in range(2):
                        at = i * (2 * N) + par * N
                        halves_multiplied(sp, i * 4 + 2 * par)
                        load_k(at, par)
                        sp.wait_ge(v_placed, i * 2 + par + 1)
                        load_v(at * H, at * H + FULL * T * H, par)
                        halves_multiplied(sp, i * 4 + 2 * par + 1)
                        load_q(at, 0)
                        sp.wait_ge(o_copied, i * 4 + 2 * par + 1)
                        sp.sem_inc(stores, 1)
                        store([at + j * QT for j in range(4)], 0)
                        halves_multiplied(sp, i * 4 + 2 * par + 2)
                        load_q(at + HALF, 1)
                        sp.wait_ge(o_copied, i * 4 + 2 * par + 2)
                        sp.sem_inc(stores, 1)
                        store([at + (HALF + j * QT) for j in range(4)], 1)
                sp.wait_ge(o_copied, 2 * HEADS + 1)
                store([HEADS * N + j * QT for j in range(4)], 0)
                sp.wait_ge(o_copied, 2 * HEADS + 2)
                store([HEADS * N + HALF + j * QT for j in range(4)], 1)
                for half in range(2):
                    sp.wait_ge(o_out[half], 64 * (HEADS + 1) + 16)

        @block.gpsimd
        def _(pool):
            with when(pool, flag):
                pool.wait_ge(ready, 2)
                pool.sem_inc(v_placed, 2)
                pool.sem_inc(weighed, 2)
                with pool.Fori(0, HEADS // 2) as i:
                    for s in range(2 * STEPS):
                        par, half, pair = s // STEPS, s % STEPS // PAIRS, s % PAIRS
                        if s % STEPS == 0:
                            pool.wait_ge(v_in[par], i * 32 + 32)
                            halves_summed(pool, i * 4 + 2 * par)
                            v = v_in_sb[:, par].rearrange("p (t h) -> p t h", h=H)
                            nc.gpsimd.tensor_tensor(v_aug[:, par, :, 0:H], v, one[:].rearrange("p (t h) -> p t h", h=H),
                                                    ALU.mult).then_inc(v_placed, 1)
                        r = rows(2 * pair)
                        p = prob[0:r, s % 2, 2 * BY_POOL * CH:2 * (BY_POOL + 1) * CH]
                        pool.wait_ge(exps, i * (6 * STEPS) + 3 * s + 5)
                        nc.gpsimd.tensor_tensor(p, p, weight[0:r, half, pair], ALU.mult).then_inc(weighed, 1)

        @block.vector
        def _(dve):
            with when(dve, flag):
                nc.vector.memset(prob[:], 0.0)
                nc.vector.memset(o_sb[:], 0.0)
                nc.vector.memset(one[:], 1.0)
                nc.vector.memset(v_in_sb[:], 0.0)
                nc.vector.memset(q_st[:], 0.0)
                nc.vector.memset(k_st[:], 1.0)
                nc.vector.memset(v_aug[:], 0.0).then_inc(ready, 1)
                dve.wait_ge(ready, 1)
                nc.vector.memset(v_aug[0:FULL, :, REST:T, H:H + 1], 1.0)
                nc.vector.memset(v_aug[0:PR, :, 0:REST, H:H + 1], 1.0).then_inc(ready, 1)
                dve.wait_ge(ready, 2)
                dve.sem_inc(added, 2)
                dve.sem_inc(o_copied, 1)

                def copy_sums(n_full, n_out, half):
                    halves_summed(dve, n_full)
                    if n_out is not None:
                        dve.wait_ge(o_out[half], n_out + 16)
                    nc.vector.tensor_copy(o_sb[:, half], O[:, half, 0:QT]).then_inc(o_copied, 1)

                with dve.Fori(0, HEADS // 2) as i:
                    for s in range(2 * STEPS):
                        par, half, pair = s // STEPS, s % STEPS // PAIRS, s % PAIRS
                        r = rows(2 * pair)
                        for u in BY_DVE:
                            dve.wait_ge(pv, i * (4 * STEPS) + PV0 + 2 * s + u)
                            dve.wait_ge(qk, i * (6 * STEPS) + QK0 + 3 * s + u + 1)
                            cols = slice(2 * u * CH, 2 * (u + 1) * CH)
                            nc.vector.scalar_tensor_tensor(
                                out=prob[0:r, s % 2, cols].rearrange("p (a b) -> p a b", b=CH),
                                in0=adj_a[0:r, half, pair, cols].rearrange("p (a b) -> p a b", b=CH), scalar=ADJ_GAIN,
                                in1=S[0:r, 2 * u:2 * u + 2, 0:CH], op0=ALU.mult, op1=ALU.add).then_inc(added, 1)
                        if pair == 1:
                            if half == 0:
                                copy_sums(i * 4 + 2 * par + 2, i * 128 + 64 * par, 1)
                            else:
                                copy_sums(i * 4 + 2 * par + 3, i * 128 + 64 * par + 64, 0)
                copy_sums(2 * HEADS + 2, 64 * HEADS, 1)

        @block.scalar
        def _(act):
            with when(act, flag):
                act.wait_ge(ready, 2)
                act.sem_inc(exps, 3)
                with act.Fori(0, HEADS // 2) as i:
                    for s in range(2 * STEPS):
                        r = rows(2 * (s % PAIRS))
                        for u in (0, BY_POOL, 1):
                            cols = slice(2 * u * CH, 2 * (u + 1) * CH)
                            p = prob[0:r, s % 2, cols]
                            if u in BY_DVE:
                                act.wait_ge(added, i * (4 * STEPS) + 2 * s + u + 3)
                                nc.scalar.activation(p, p, ACT.Exp).then_inc(exps, 1)
                            else:
                                act.wait_ge(qk, i * (6 * STEPS) + QK0 + 3 * s + u + 1)
                                nc.scalar.activation(p.rearrange("p (a b) -> p a b", b=CH),
                                                     S[0:r, 2 * u:2 * u + 2, 0:CH], ACT.Exp).then_inc(exps, 1)

        @block.tensor
        def _(pe):
            with when(pe, flag):
                pe.wait_ge(ready, 2)
                pe.sem_inc(qk, QK0)
                pe.sem_inc(pv, PV0)

                def scores(i, s, u):
                    par, half, pair = s // STEPS, s % STEPS // PAIRS, s % PAIRS
                    if pair == 0 and u == 0:
                        pe.wait_ge(q_in[half], i * 192 + 96 * (par + 1))
                        if half == 0:
                            pe.wait_ge(k_in[par], i * 48 + 48)
                    if u in BY_DVE:
                        pe.wait_ge(added, i * (4 * STEPS) + 2 * s + u + 1)
                    else:
                        pe.wait_ge(exps, i * (6 * STEPS) + 3 * s + 2)
                    for c in (2 * u, 2 * u + 1):
                        t, cols = 2 * pair + c // 3, slice(c % 3 * CH, (c % 3 + 1) * CH)
                        r = rows(t)
                        last = nc.tensor.matmul(S[0:r, c, 0:CH], k_st[:, par, t:t + T * (r - 1) + 1:T],
                                                q_st[:, half, cols], start=True, stop=True)
                    last.then_inc(qk, 1)

                def sums(i, s, j):
                    par, half, pair = s % (2 * STEPS) // STEPS, s % STEPS // PAIRS, s % PAIRS
                    t = 2 * pair + j
                    if j == 0:
                        pe.wait_ge(exps, i * (6 * STEPS) + 3 * s + 6)
                    else:
                        pe.wait_ge(weighed, i * (2 * STEPS) + s + 3)
                    if t == 0:
                        pe.wait_ge(o_copied, i * 4 + 2 * par + 1 + half)
                        if half == 0:
                            pe.wait_ge(v_placed, i * 2 + par + 3)
                    r = rows(t)
                    for g in range(4):
                        last = nc.tensor.matmul(O[32 * g:32 * g + 32, half, 0:QT], v_aug[0:r, par, t, :],
                                                prob[0:r, s % 2, j * HALF + g * QT:j * HALF + (g + 1) * QT],
                                                start=(t == 0), stop=(t == T - 1))
                    last.then_inc(pv, 1)

                for g in range(4):
                    nc.tensor.matmul(O[32 * g:32 * g + 32, 1, 0:QT], v_aug[0:FULL, 1, 0, :], prob[0:FULL, 1, 0:QT],
                                     start=True, stop=False)
                with pe.Fori(0, HEADS // 2) as i:
                    for s in range(2 * STEPS):
                        scores(i, s, 0)
                        scores(i, s, 1)
                        sums(i, s - 2, 1)
                        scores(i, s, 2)
                        sums(i, s - 1, 0)
                sums(HEADS // 2, -2, 1)
                sums(HEADS // 2, -1, 0)
                sums(HEADS // 2, -1, 1)


def check_sums(nc, dram, flag):
    with ExitStack() as ctx:
        def sb(name, shape, dt=F32):
            return ctx.enter_context(nc.sbuf_tensor(name, shape, dt))

        def sem(name):
            return ctx.enter_context(nc.semaphore(name))

        den = sb("den", [128, N])
        fit = sb("fit", [128, N])
        worst = sb("worst", [128, 2])
        den_in = sem("den_in")
        step = sem("step_c")
        spread = sem("spread")
        block = ctx.enter_context(nc.Block())

        @block.sync
        def _(sp):
            sp.dma_start(den[:], dram["od"][H, N:N + G].rearrange("(p c) -> p c", c=N)).then_inc(den_in, 16)

        @block.vector
        def _(dve):
            dve.wait_ge(den_in, 16)
            nc.vector.tensor_scalar(fit[:], den[:], LEAST, 1e30, ALU.max, ALU.min).then_inc(step, 1)
            dve.wait_ge(step, 1)
            nc.vector.tensor_tensor(fit[:], fit[:], den[:], ALU.not_equal).then_inc(step, 1)
            dve.wait_ge(step, 2)
            nc.vector.tensor_reduce(worst[:, 0:1], fit[:], AX.X, ALU.max).then_inc(step, 1)
            dve.wait_ge(spread, 1)
            nc.vector.tensor_copy(flag[:], worst[:, 1:2]).then_inc(step, 1)
            dve.wait_ge(step, 4)

        @block.gpsimd
        def _(pool):
            pool.wait_ge(step, 3)
            nc.gpsimd.partition_all_reduce(worst[:, 1:2], worst[:, 0:1], 128, bass.bass_isa.ReduceOp.max).then_inc(spread, 1)


def true_guards(nc, dram, keep, flag):
    ident = keep["ident"]
    with ExitStack() as ctx:
        def sb(name, shape, dt=F32):
            return ctx.enter_context(nc.sbuf_tensor(name, shape, dt))

        def sem(name):
            return ctx.enter_context(nc.semaphore(name))

        q_st = sb("q_max", [TERMS, 128 * NB], BF16)
        k_st = sb("k_max", [TERMS, N], BF16)
        two = sb("two", [128, NB, 2])
        top = sb("top", [128, NB])
        guard = sb("guard", [NB, 2, 128], BF16)
        ps = ctx.enter_context(nc.psum_tensor("ps_max", [128, 8, 512], F32))
        qk_in = sem("qk_in")
        mult = sem("mult")
        reduced = sem("reduced")
        topped = sem("topped")
        turned = sem("turned_m")
        halved = sem("halved")
        stores = sem("stores_m")
        written = sem("written")
        block = ctx.enter_context(nc.Block())
        LAST = N - 5 * CH

        @block.sync
        def _(sp):
            with when(sp, flag):
                with sp.Fori(0, HEADS) as h:
                    at = h * N
                    cols = bass.ds(at, N)
                    qd, kd = dram["qd"], dram["kd"]
                    for r0, n in ((0, 24), (24, 16), (40, 8)):
                        sp.dma_start(k_st[r0:r0 + n], kd[0:n, cols]).then_inc(qk_in, 16)
                    for r0, p in ((0, 0), (8, 0), (16, 0), (24, 1), (32, 1), (40, 2)):
                        sp.dma_start(q_st[r0:r0 + 8, 0:N], qd[8 * p:8 * p + 8, cols]).then_inc(qk_in, 16)
                    whole = 128 * (NB - 1)
                    firsts = bass.ds(at, whole)
                    rest = bass.ds(at + whole, N - whole)
                    sp.wait_ge(halved, h * 2 + 2)
                    sp.sem_inc(stores, 1)
                    for j in range(2):
                        sp.dma_start(qd[24 + j, firsts].rearrange("(b c) -> b c", c=128), guard[0:NB - 1, j])\
                          .then_inc(written, 16)
                        sp.dma_start(qd[24 + j:25 + j, rest], guard[NB - 1:NB, j, 0:N - whole]).then_inc(written, 16)
                    sp.wait_ge(written, h * 64 + 64)
                    sp.sem_inc(stores, 1)

        @block.tensor
        def _(pe):
            with when(pe, flag):
                with pe.Fori(0, HEADS) as h:
                    pe.wait_ge(qk_in, h * 144 + 144)
                    pe.wait_ge(topped, h * 2 + 1)
                    for b in range(NB):
                        pe.wait_ge(reduced, h * NB + b + 1)
                        for c in range(6):
                            w = CH if c < 5 else LAST
                            last = nc.tensor.matmul(ps[:, c, 0:w], q_st[:, 128 * b:128 * (b + 1)],
                                                    k_st[:, c * CH:c * CH + w], start=True, stop=True)
                        last.then_inc(mult, 1)
                    pe.wait_ge(topped, h * 2 + 3)
                    nc.tensor.transpose(ps[0:NB, 6, 0:128], top[:], ident[:]).then_inc(turned, 1)

        @block.vector
        def _(dve):
            with when(dve, flag):
                nc.vector.memset(q_st[:, N:], 0.0).then_inc(topped, 1)
                dve.wait_ge(topped, 1)
                dve.sem_inc(reduced, 1)
                with dve.Fori(0, HEADS) as h:
                    for b in range(NB):
                        dve.wait_ge(mult, h * NB + b + 1)
                        nc.vector.tensor_reduce(two[:, b, 0:1], ps[:, 0:5, 0:CH], AX.XY, ALU.max)
                        nc.vector.tensor_reduce(two[:, b, 1:2], ps[:, 5, 0:LAST], AX.X, ALU.max).then_inc(reduced, 1)
                    dve.wait_ge(reduced, h * NB + NB + 1)
                    nc.vector.tensor_reduce(top[:], two[:], AX.X, ALU.max).then_inc(topped, 1)
                    dve.wait_ge(topped, h * 2 + 2)
                    nc.vector.tensor_scalar(top[:], top[:], -1.0, -ADJ_GAIN, ALU.mult, ALU.add).then_inc(topped, 1)
                    dve.wait_ge(turned, h + 1)
                    nc.vector.tensor_copy(guard[:, 0], ps[0:NB, 6, 0:128]).then_inc(halved, 1)
                    dve.wait_ge(halved, h * 2 + 1)
                    nc.vector.tensor_tensor(guard[:, 1], ps[0:NB, 6, 0:128], guard[:, 0], ALU.subtract).then_inc(halved, 1)


def finish(nc, dram, keep):
    ident = keep["ident"]
    with ExitStack() as ctx:
        def sb(name, shape, dt=F32):
            return ctx.enter_context(nc.sbuf_tensor(name, shape, dt))

        def sem(name):
            return ctx.enter_context(nc.semaphore(name))

        wo = sb("wo", [D, H, D])
        z = sb("z", [128, 3, H + 1, D])
        y1 = sb("y1", [128, 3, D])
        zT = sb("zT", [128, 2, H * 128])
        res = sb("res", [128, 2, D])
        st = sb("st", [128, 2, 6])
        mv = sb("mv_f", [128, 2, 2])
        rs = sb("rs", [128, 2])
        ps = ctx.enter_context(nc.psum_tensor("ps2", [128, 8, 512], F32))
        w_in = sem("wo_in")
        z_in = [sem(f"z_in{j}") for j in range(3)]
        divided = sem("divided")
        turned = sem("turned_f")
        placed = sem("placed_f")
        out_mm = sem("out_mm")
        added = sem("added_f")
        rooted = sem("rooted_f")
        normed = sem("normed_f")
        out_done = [sem(f"out_done{j}") for j in range(2)]
        chain = sem("chain_f")
        block = ctx.enter_context(nc.Block())
        size = [min(128, N - 128 * b) for b in range(NB)]

        @block.sync
        def _(sp):
            sp.dma_start(wo[:], dram["wo"]).then_inc(w_in, 16)
            for b in range(NB):
                if b >= 3:
                    sp.wait_ge(normed, b - 2)
                at = N + 128 * 128 * b
                sp.dma_start(z[0:size[b], b % 3], dram["od"][:, at:at + 128 * size[b]].rearrange("r (i c) -> i r c", c=D))\
                  .then_inc(z_in[b % 3], 16)
                sp.dma_start(y1[0:size[b], b % 3], dram["y1"][128 * b:128 * b + size[b]]).then_inc(z_in[b % 3], 16)

        @block.gpsimd
        def _(pool):
            for b in range(NB):
                pool.wait_ge(normed, b + 1)
                pool.dma_start(dram["out"][128 * b:128 * b + size[b]], res[0:size[b], b % 2]).then_inc(out_done[b % 2], 16)
            for j in range(2):
                pool.wait_ge(out_done[j], 16 * (NB // 2))

        @block.tensor
        def _(pe):
            def turn(b):
                n = size[b]
                pe.wait_ge(divided, b + 1)
                if b >= 2:
                    pe.wait_ge(placed, b - 1)
                for h in range(H):
                    last = nc.tensor.transpose(ps[:, 2 * (b % 2) + h // 4, (h % 4) * 128:(h % 4) * 128 + n],
                                               z[0:n, b % 3, h, :], ident[0:n, 0:n])
                last.then_inc(turned, 1)

            def out(b):
                n = size[b]
                pe.wait_ge(placed, b + 1)
                if b >= 2:
                    pe.wait_ge(added, b - 1)
                for h in range(H):
                    last = nc.tensor.matmul(ps[0:n, 4 + b % 2, 0:D], zT[:, b % 2, h * 128:h * 128 + n], wo[:, h, :],
                                            start=(h == 0), stop=(h == H - 1))
                last.then_inc(out_mm, 1)

            pe.wait_ge(w_in, 16)
            turn(0)
            for b in range(1, NB):
                turn(b)
                out(b - 1)
            out(NB - 1)

        @block.scalar
        def _(act):
            for b in range(NB):
                n = size[b]
                act.wait_ge(turned, b + 1)
                if b >= 2:
                    act.wait_ge(out_mm, b - 1)
                nc.scalar.copy(zT[:, b % 2].rearrange("p (a h n) -> p a h n", a=2, n=128)[:, :, :, 0:n],
                               ps[:, 2 * (b % 2):2 * (b % 2) + 2, :].rearrange("p a (h n) -> p a h n", n=128)[:, :, :, 0:n])\
                  .then_inc(placed, 1)
                act.wait_ge(added, b + 1)
                nc.scalar.activation(rs[0:n, b % 2:b % 2 + 1], rs[0:n, b % 2:b % 2 + 1], ACT.Sqrt).then_inc(rooted, 1)

        @block.vector
        def _(dve):
            links = [0]

            def link(ins):
                links[0] += 1
                ins.then_inc(chain, 1)
                dve.wait_ge(chain, links[0])

            def divide(b):
                n = size[b]
                dve.wait_ge(z_in[b % 3], 32 * (b // 3 + 1))
                link(nc.vector.reciprocal(z[0:n, b % 3, H], z[0:n, b % 3, H]))
                nc.vector.tensor_tensor(z[0:n, b % 3, 0:H], z[0:n, b % 3, 0:H],
                                        z[0:n, b % 3, H:H + 1].broadcast_to((n, H, D)), ALU.mult).then_inc(divided, 1)

            divide(0)
            for b in range(NB):
                n, j = size[b], b % 2
                if b + 1 < NB:
                    divide(b + 1)
                dve.wait_ge(out_mm, b + 1)
                if b >= 2:
                    dve.wait_ge(out_done[j], 16 * (b // 2))
                link(nc.vector.tensor_tensor(res[0:n, j], ps[0:n, 4 + j, 0:D], y1[0:n, b % 3], ALU.add))
                link(nc.vector.bn_stats(st[0:n, j], res[0:n, j]))
                link(nc.vector.bn_aggr(mv[0:n, j], st[0:n, j]))
                nc.vector.tensor_scalar(rs[0:n, j:j + 1], mv[0:n, j, 1:2], EPS, None, ALU.add).then_inc(added, 1)
                dve.wait_ge(rooted, b + 1)
                link(nc.vector.reciprocal(rs[0:n, j:j + 1], rs[0:n, j:j + 1]))
                nc.vector.tensor_scalar(res[0:n, j], res[0:n, j], mv[0:n, j, 0:1], rs[0:n, j:j + 1],
                                        ALU.subtract, ALU.mult).then_inc(normed, 1)


def adj_attention_kernel(nc, x, adjT, W, b, wq, wk, wv, wo, out):
    def scratch(name, shape, dt=F32):
        return nc.dram_tensor(name, shape, dt, kind="Internal").ap()

    dram = {"x": x, "adjT": adjT, "W": W, "b": b, "wq": wq, "wk": wk, "wv": wv, "wo": wo, "out": out,
            "y1": scratch("y1_d", [N, D]), "qd": scratch("q_d", [26, G], BF16), "kd": scratch("k_d", [24, G], BF16),
            "vd": scratch("v_d", [N, CW]), "od": scratch("o_d", [H + 1, N + G])}
    with ExitStack() as ctx:
        weight = ctx.enter_context(nc.sbuf_tensor("weight", [128, 2, PAIRS, 2 * CH], F32))
        flat = weight[:].rearrange("p h a n -> p (h a n)")
        half = 2 * PAIRS * CH
        keep = {"adj_a": ctx.enter_context(nc.sbuf_tensor("adj_a", [PR, 2, PAIRS, 4 * CH], BF16)),
                "ident": ctx.enter_context(nc.sbuf_tensor("ident", [128, 128], F32)),
                "weight": weight,
                "spare": flat[:, 0:half],
                "adj_b": flat[0:PR, half:].bitcast(BF16).rearrange("p (h a n) -> p h a n", h=2, a=PAIRS)}
        with nc.sbuf_tensor("yT", [D, T * PR], F32) as yT:
            keep["yT"] = yT
            layer0(nc, dram, keep)
            project(nc, dram, keep)
        weigh(nc, keep)
        attend(nc, dram, keep, "")
        with nc.sbuf_tensor("flag", [128, 1], I32) as flag:
            check_sums(nc, dram, flag)
            true_guards(nc, dram, keep, flag)
            attend(nc, dram, keep, "_again", flag)
        finish(nc, dram, keep)


def kernel(**inputs):
    import numpy as _np
    import concourse.bacc as _bacc
    from concourse import mybir as _mybir
    from concourse.bass_utils import run_bass_kernel_spmd as _run

    def turned(name):
        return _np.ascontiguousarray(_np.asarray(inputs[name]).T)

    def by_column(name):
        w = _np.asarray(inputs[name])
        return _np.ascontiguousarray(w.reshape(D, H, D).transpose(2, 1, 0)).reshape(D, CW)

    given = {
        "x": _np.ascontiguousarray(inputs["x"]), "adjT": turned("adj"),
        "W": _np.ascontiguousarray(inputs["L0_gnn_W"]), "b": _np.ascontiguousarray(inputs["L0_gnn_b"]),
        "wq": by_column("L1_gnn_Wq"), "wk": by_column("L1_gnn_Wk"), "wv": turned("L1_gnn_Wv"),
        "wo": turned("L1_gnn_Wo").reshape(D, H, D),
    }
    nc = _bacc.Bacc("TRN2", target_bir_lowering=False, num_devices=1)
    arrays, args = {}, []
    for name, a in given.items():
        arrays[f"in_{name}_dram"] = a
        args.append(nc.dram_tensor(f"in_{name}_dram", a.shape, _mybir.dt.from_np(a.dtype), kind="ExternalInput").ap())
    args.append(nc.dram_tensor("out_0_dram", (N, D), _mybir.dt.float32, kind="ExternalOutput").ap())
    adj_attention_kernel(nc, *args)
    r = _run(nc, [arrays], core_ids=[0])
    return r.results[0]["out_0_dram"]
```

```python
from contextlib import ExitStack

import concourse.bass as bass
from concourse import mybir

F32 = mybir.dt.float32
BF16 = mybir.dt.bfloat16
I32 = mybir.dt.int32
ALU = mybir.AluOpType
ACT = mybir.ActivationFunctionType
AX = mybir.AxisListType

N = 2708
D = 128
H = 8
T = 22
FULL = N // T
REST = N - FULL * T
PR = FULL + 1
CH = 452
HALF = 3 * CH
NP = 2 * HALF
QT = HALF // 4
CW = H * D
G = N * D
PAIRS = T // 2
STEPS = 2 * PAIRS
NB = -(-N // 128)
TERMS = 6 * H
ROWS = TERMS + 2
SCALE = float(D) ** -0.5
EPS = 1e-5
ADJ_GAIN = 2.0
HEADS = D
BY_DVE = (0, 1)
LEAST = 2.0 ** -64
QK_HALF = 3 * PAIRS


def chunk(keep, r, half, t, c):
    i = 3 * (t % 2) + c
    if i < 4:
        return keep["adj_a"][0:r, half, t // 2, i * CH:(i + 1) * CH]
    return keep["adj_b"][0:r, half, t // 2, (i - 4) * CH:(i - 3) * CH]


def rows(t):
    return PR if t < REST else FULL


def layer0(nc, dram, keep):
    x, adjT, W, b = dram["x"], dram["adjT"], dram["W"], dram["b"]
    adj_a, adj_b, yT, ident = keep["adj_a"], keep["adj_b"], keep["yT"], keep["ident"]
    with ExitStack() as ctx:
        def sb(name, shape, dt=F32):
            return ctx.enter_context(nc.sbuf_tensor(name, shape, dt))

        def sem(name):
            return ctx.enter_context(nc.semaphore(name))

        xs = sb("xs", [PR, T, D])
        part = [sb(f"part{k}", [PR, T, D], BF16) for k in range(3)]
        x1 = keep["spare"][0:PR, 0:T * D].rearrange("p (t d) -> p t d", d=D)
        nT = yT
        w_sb = sb("w_sb", [D, D])
        b_sb = sb("b_sb", [1, D])
        ones_row = sb("ones_row", [1, 128])
        tmp = keep["spare"][0:PR, T * D:(T + 4) * D].rearrange("p (t d) -> p t d", d=D)
        stats = sb("stats", [PR, T, 6])
        mv = sb("mv", [PR, T, 2])
        rstd = sb("rstd", [PR, T])
        ps = ctx.enter_context(nc.psum_tensor("ps0", [128, 8, 512], F32))

        id_made = sem("id_made")
        pads = sem("pads")
        x_in = sem("x_in")
        w_in = sem("w_in")
        adj_in = [sem(f"adj_in{t}") for t in range(T)]
        split_vec = sem("split_vec")
        split_act = sem("split_act")
        summed = sem("summed")
        copied_v = sem("copied_v")
        copied_a = sem("copied_a")
        lin = sem("lin")
        clamped = sem("clamped")
        expd = sem("expd")
        chain = sem("chain")
        swished = sem("swished")
        varred = sem("varred")
        rooted = sem("rooted")
        normed = sem("normed")
        turned = sem("turned")
        placed = sem("placed")
        y_out = sem("y_out")
        GROUPS = [(g, min(4, T - g)) for g in range(0, T, 4)]
        block = ctx.enter_context(nc.Block())

        @block.sync
        def _(sp):
            sp.dma_start(w_sb[:], W).then_inc(w_in, 16)
            sp.dma_start(b_sb[:], b.rearrange("(a d) -> a d", a=1)).then_inc(w_in, 16)
            sp.wait_ge(pads, 1)
            sp.dma_start(xs[0:FULL], x[0:FULL * T].rearrange("(p t) d -> p t d", t=T)).then_inc(x_in, 16)
            sp.dma_start(xs[FULL:PR, 0:REST], x[FULL * T:N].rearrange("(p t) d -> p t d", t=REST)).then_inc(x_in, 16)
            sp.wait_ge(normed, T)
            y1 = dram["y1"]
            sp.dma_start(y1[0:FULL * T].rearrange("(p t) d -> p t d", t=T), xs[0:FULL]).then_inc(y_out, 16)
            sp.dma_start(y1[FULL * T:N].rearrange("(p t) d -> p t d", t=REST), xs[FULL:PR, 0:REST]).then_inc(y_out, 16)
            sp.wait_ge(y_out, 32)

        @block.gpsimd
        def _(pool):
            nc.gpsimd.memset(ident[:], 0.0).then_inc(id_made, 1)
            pool.wait_ge(id_made, 1)
            nc.gpsimd.affine_select(out=ident[:], in_=ident[:], compare_op=ALU.not_equal, fill=1.0, base=0,
                                    pattern=[[-1, 128]], channel_multiplier=1).then_inc(id_made, 1)
            whole = adjT[0:FULL * T].rearrange("(p t) n -> p t n", t=T)
            for t in range(T):
                for half in range(2):
                    n0, n1 = half * HALF, min(N, (half + 1) * HALF)
                    if t % 2 == 0:
                        pieces = [(adj_a, 0, n0, n1)]
                    else:
                        pieces = [(adj_a, 3 * CH, n0, n0 + CH), (adj_b, 0, n0 + CH, n1)]
                    for to, at, lo, hi in pieces:
                        pool.dma_start(to[0:FULL, half, t // 2, at:at + hi - lo], whole[:, t, lo:hi]).then_inc(adj_in[t], 16)
                        if t < REST:
                            pool.dma_start(to[FULL:PR, half, t // 2, at:at + hi - lo],
                                           adjT[FULL * T + t:FULL * T + t + 1, lo:hi]).then_inc(adj_in[t], 16)

        def aggregate(pe, first):
            for t in range(T):
                if first:
                    pe.wait_ge(adj_in[t], 32 * (1 + t % 2) * (2 if t < REST else 1))
                for k in range(3):
                    for c in range(6):
                        last = nc.tensor.matmul(ps[:, c, 0:CH], part[k][0:rows(t), t, :],
                                                chunk(keep, rows(t), c // 3, t, c % 3),
                                                start=(t == 0 and k == 0), stop=(t == T - 1 and k == 2))
            last.then_inc(summed, 1)

        def linear(pe, rnd):
            pe.wait_ge(copied_v, 3 * (rnd + 1))
            pe.wait_ge(copied_a, 3 * (rnd + 1))
            for i, (g, n) in enumerate(GROUPS):
                if i >= 2 or rnd:
                    pe.wait_ge(swished, rnd * len(GROUPS) + i - 1)
                for j in range(n):
                    nc.tensor.matmul(ps[0:PR, 6 + i % 2, j * D:(j + 1) * D],
                                     nT[:, g + j:g + j + T * (PR - 1) + 1:T], w_sb[:], start=True, stop=False)
                    last = nc.tensor.matmul(ps[0:PR, 6 + i % 2, j * D:(j + 1) * D], ones_row[0:1, 0:PR], b_sb[:],
                                            start=False, stop=True)
                last.then_inc(lin, 1)

        @block.tensor
        def _(pe):
            pe.wait_ge(split_act, 2)
            pe.wait_ge(split_vec, 2)
            aggregate(pe, True)
            pe.wait_ge(w_in, 32)
            pe.wait_ge(pads, 2)
            linear(pe, 0)
            pe.wait_ge(split_act, 4)
            pe.wait_ge(split_vec, 4)
            aggregate(pe, False)
            linear(pe, 1)
            pe.wait_ge(id_made, 2)
            for i, (g, n) in enumerate(GROUPS):
                pe.wait_ge(normed, g + n)
                if i >= 2:
                    pe.wait_ge(placed, i - 1)
                for j in range(n):
                    last = nc.tensor.transpose(ps[:, 4 + i % 2, j * D:j * D + PR], xs[0:PR, g + j, :], ident[0:PR, 0:PR])
                last.then_inc(turned, 1)

        @block.scalar
        def _(act):
            act.wait_ge(x_in, 32)
            for rnd in range(2):
                if rnd:
                    act.wait_ge(swished, len(GROUPS))
                    act.wait_ge(summed, 1)
                nc.scalar.copy(part[0][:], xs[:] if rnd == 0 else x1).then_inc(split_act, 1)
                act.wait_ge(split_vec, 2 * rnd + 1)
                nc.scalar.copy(part[1][:], x1).then_inc(split_act, 1)
                act.wait_ge(summed, rnd + 1)
                for c in range(3):
                    w = min(CH, N - c * CH)
                    nc.scalar.copy(nT[:, c * CH:c * CH + w], ps[:, c, 0:w]).then_inc(copied_a, 1)
                for i, (g, n) in enumerate(GROUPS):
                    act.wait_ge(clamped, rnd * len(GROUPS) + i + 1)
                    nc.scalar.activation(tmp[:, 0:n], tmp[:, 0:n], ACT.Exp, scale=-1.0).then_inc(expd, 1)
            act.wait_ge(varred, 1)
            nc.scalar.activation(rstd[:], rstd[:], ACT.Sqrt).then_inc(rooted, 1)

        @block.vector
        def _(dve):
            links = [0]

            def link(ins):
                links[0] += 1
                ins.then_inc(chain, 1)
                dve.wait_ge(chain, links[0])

            nc.vector.memset(xs[:], 0.0).then_inc(pads, 1)
            link(nc.vector.memset(nT[:, N:], 0.0))
            link(nc.vector.memset(adj_a[:, 1, :, 3 * CH - (NP - N):3 * CH], 0.0))
            link(nc.vector.memset(adj_b[:, 1, :, 2 * CH - (NP - N):2 * CH], 0.0))
            nc.vector.memset(ones_row[:], 1.0).then_inc(pads, 1)
            dve.wait_ge(x_in, 32)
            for rnd in range(2):
                src = xs[:] if rnd == 0 else x1
                dve.wait_ge(split_act, 2 * rnd + 1)
                nc.vector.tensor_tensor(x1, src, part[0][:], ALU.subtract).then_inc(split_vec, 1)
                dve.wait_ge(split_vec, 2 * rnd + 1)
                dve.wait_ge(split_act, 2 * rnd + 2)
                if rnd:
                    dve.wait_ge(summed, 1)
                nc.vector.tensor_tensor(part[2][:], x1, part[1][:], ALU.subtract).then_inc(split_vec, 1)
                dve.wait_ge(summed, rnd + 1)
                for c in range(3, 6):
                    w = min(CH, N - c * CH)
                    nc.vector.tensor_copy(nT[:, c * CH:c * CH + w], ps[:, c, 0:w]).then_inc(copied_v, 1)
                if rnd == 0:
                    dve.wait_ge(split_vec, 2)
                for i, (g, n) in enumerate(GROUPS):
                    dve.wait_ge(lin, rnd * len(GROUPS) + i + 1)
                    z = ps[0:PR, 6 + i % 2, 0:n * D].rearrange("p (j d) -> p j d", d=D)
                    nc.vector.tensor_scalar(tmp[:, 0:n], z, -80.0, None, ALU.max).then_inc(clamped, 1)
                    dve.wait_ge(expd, rnd * len(GROUPS) + i + 1)
                    link(nc.vector.tensor_scalar(tmp[:, 0:n], tmp[:, 0:n], 1.0, None, ALU.add))
                    link(nc.vector.reciprocal(tmp[:, 0:n], tmp[:, 0:n]))
                    nc.vector.tensor_tensor(x1[:, g:g + n], z, tmp[:, 0:n], ALU.mult).then_inc(swished, 1)
                    dve.wait_ge(swished, rnd * len(GROUPS) + i + 1)
            link(nc.vector.tensor_tensor(xs[:], xs[:], x1, ALU.add))
            for t in range(T):
                last = nc.vector.bn_stats(stats[:, t], xs[:, t])
            link(last)
            for t in range(T):
                last = nc.vector.bn_aggr(mv[:, t], stats[:, t])
            link(last)
            nc.vector.tensor_scalar(rstd[:], mv[:, :, 1], EPS, None, ALU.add).then_inc(varred, 1)
            dve.wait_ge(rooted, 1)
            link(nc.vector.reciprocal(rstd[:], rstd[:]))
            for t in range(T):
                nc.vector.tensor_scalar(xs[:, t], xs[:, t], mv[:, t, 0:1], rstd[:, t:t + 1],
                                        ALU.subtract, ALU.mult).then_inc(normed, 1)
            yT_tiles = yT[:].rearrange("d (p t) -> d t p", t=T)
            for i, (g, n) in enumerate(GROUPS):
                dve.wait_ge(turned, i + 1)
                nc.vector.tensor_copy(yT_tiles[:, g:g + n, 0:PR],
                                      ps[:, 4 + i % 2, 0:n * D].rearrange("p (j d) -> p j d", d=D)[:, :, 0:PR]).then_inc(placed, 1)
            dve.wait_ge(placed, len(GROUPS))


def project(nc, dram, keep):
    yT = keep["yT"]
    with ExitStack() as ctx:
        def sb(name, shape, dt=F32):
            return ctx.enter_context(nc.sbuf_tensor(name, shape, dt))

        def sem(name):
            return ctx.enter_context(nc.semaphore(name))

        def spare(at, a, c):
            return keep["spare"][0:PR, at:at + a * c].rearrange("p (a c) -> p a c", c=c)

        w = {c: sb(f"w{c}", [D, CW]) for c in "kqv"}
        parts = sb("parts", [PR, 2, 24, 2, D], BF16)
        rem = spare(0, 2, CW)
        sq = spare(2 * CW, 2, CW)
        v_sb = spare(4 * CW, 2, CW)
        bound = spare(6 * CW, T, D)
        guard = keep["spare"][0:PR, 0:T * D].bitcast(BF16).rearrange("p (a t c) -> p a t c", a=2, c=D)
        ksq = sb("ksq", [PR, D])
        kmax = sb("kmax", [128, T])
        kall = sb("kall", [128, 2])
        ps = ctx.enter_context(nc.psum_tensor("ps1", [128, 8, 512], F32))

        w_in = [sem(f"w_in_{c}") for c in "kqv"]
        proj = sem("proj")
        projv = sem("projv")
        high = sem("high")
        sqd = sem("sqd")
        remd = sem("remd")
        mid = sem("mid")
        low = sem("low")
        nsqd = sem("nsqd")
        maxd = sem("maxd")
        allmax = sem("allmax")
        rooted = sem("rooted")
        guard_steps = sem("guard_steps")
        v_cp = sem("v_cp")
        stored = [sem(f"stored{j}") for j in range(2)]
        v_out = [sem(f"v_out{j}") for j in range(2)]
        guard_out = sem("guard_out")
        block = ctx.enter_context(nc.Block())
        jobs = [("k", t) for t in range(T)] + [("q", t) for t in range(T)]

        def buffer(i):
            return parts[:, (i // 2) % 2, :, i % 2, :]

        def stored_by(u):
            return 16 * sum(2 if v % PAIRS == 0 else 1 for v in range(u % 2, u + 1, 2))

        def v_out_by(t):
            return 16 * (t // 2 + 2)

        @block.sync
        def _(sp):
            for c, s in zip("kqv", w_in):
                sp.dma_start(w[c][:], dram["w" + c]).then_inc(s, 16)
            for i, (c, t) in enumerate(jobs):
                if t % 2:
                    sp.wait_ge(low, i + 1)
                    u, d = i // 2, dram[c + "d"]
                    sp.dma_start(d[0:24, 0:FULL * T * D].rearrange("r (p n) -> p r n", p=FULL)[:, :, (t - 1) * D:(t + 1) * D],
                                 parts[0:FULL, u % 2].rearrange("p r t c -> p r (t c)")).then_inc(stored[u % 2], 16)
                    if t < REST:
                        sp.dma_start(d[0:24, FULL * T * D:G].rearrange("r (p n) -> p r n", p=1),
                                     parts[FULL:PR, u % 2].rearrange("p r t c -> p r (t c)")).then_inc(stored[u % 2], 16)
                if c == "q":
                    sp.wait_ge(v_cp, t + 1)
                    sp.dma_start(dram["vd"][0:FULL * T].rearrange("(p t) c -> p t c", t=T)[:, t], v_sb[0:FULL, t % 2])\
                      .then_inc(v_out[t % 2], 16)
                    if t < REST:
                        sp.dma_start(dram["vd"][FULL * T + t:FULL * T + t + 1], v_sb[FULL:PR, t % 2])\
                          .then_inc(v_out[t % 2], 16)
            sp.wait_ge(guard_steps, 3)
            for j in range(2):
                row = dram["qd"][24 + j]
                sp.dma_start(row[0:FULL * T * D].rearrange("(p n) -> p n", p=FULL),
                             guard[0:FULL, j].rearrange("p t c -> p (t c)")).then_inc(guard_out, 16)
                sp.dma_start(row[FULL * T * D:G].rearrange("(p n) -> p n", p=1),
                             guard[FULL:PR, j, 0:REST].rearrange("p t c -> p (t c)")).then_inc(guard_out, 16)
            sp.wait_ge(guard_out, 64)
            for j in range(2):
                sp.wait_ge(stored[j], stored_by(2 * PAIRS - 2 + j))
                sp.wait_ge(v_out[j], v_out_by(T - 2 + j))

        @block.tensor
        def _(pe):
            def go(c, t, bank):
                for j in range(2):
                    last = nc.tensor.matmul(ps[0:PR, bank + j, :], yT[:, t:t + T * (PR - 1) + 1:T],
                                            w[c][:, 512 * j:512 * (j + 1)], start=True, stop=True)
                return last

            for i, (c, t) in enumerate(jobs):
                if t == 0:
                    pe.wait_ge(w_in["kqv".index(c)], 16)
                if i >= 2:
                    pe.wait_ge(remd, i - 1)
                    pe.wait_ge(sqd, i - 1)
                go(c, t, 2 * (i % 2)).then_inc(proj, 1)
                if c == "q":
                    if t == 0:
                        pe.wait_ge(w_in[2], 16)
                    if t >= 2:
                        pe.wait_ge(v_cp, t - 1)
                    go("v", t, 4 + 2 * (t % 2)).then_inc(projv, 1)

        def bank(i):
            return ps[0:PR, 2 * (i % 2):2 * (i % 2) + 2, :].rearrange("p a b -> p (a b)")

        def by_row(tile):
            return tile.rearrange("p (r c) -> p r c", c=D)

        @block.scalar
        def _(act):
            for i, (c, t) in enumerate(jobs):
                sc = SCALE if c == "q" else 1.0
                act.wait_ge(proj, i + 1)
                if i >= 4 and i % 2 == 0:
                    act.wait_ge(stored[(i // 2) % 2], stored_by(i // 2 - 2))
                nc.scalar.activation(buffer(i)[:, 0:8], by_row(bank(i)), ACT.Copy, scale=sc).then_inc(high, 1)
                if i >= 2:
                    act.wait_ge(nsqd, i - 1)
                nc.scalar.activation(sq[:, i % 2], bank(i), ACT.Square, scale=sc).then_inc(sqd, 1)
                if c == "q":
                    act.wait_ge(projv, t + 1)
                    if t >= 2:
                        act.wait_ge(v_out[t % 2], v_out_by(t - 2))
                    nc.scalar.copy(v_sb[:, t % 2],
                                   ps[0:PR, 4 + 2 * (t % 2):6 + 2 * (t % 2), :].rearrange("p a b -> p (a b)")).then_inc(v_cp, 1)
            act.wait_ge(allmax, 1)
            act.wait_ge(nsqd, len(jobs))
            nc.scalar.activation(bound, bound, ACT.Sqrt, scale=kall[0:PR, 1:2]).then_inc(rooted, 1)

        @block.vector
        def _(dve):
            nc.vector.memset(kmax[:], 0.0).then_inc(maxd, 1)
            dve.wait_ge(maxd, 1)
            for i, (c, t) in enumerate(jobs):
                sc = SCALE if c == "q" else 1.0
                dve.wait_ge(sqd, i + 1)
                if i >= 2:
                    dve.wait_ge(low, i - 1)
                nc.vector.scalar_tensor_tensor(out=by_row(rem[:, i % 2]), in0=by_row(bank(i)), scalar=sc,
                                               in1=buffer(i)[:, 0:8], op0=ALU.mult, op1=ALU.subtract).then_inc(remd, 1)
                if c == "k" and t >= 1:
                    dve.wait_ge(maxd, t + 1)
                lengths = ksq[:] if c == "k" else bound[:, t]
                nc.vector.tensor_reduce(lengths, sq[:, i % 2].rearrange("p (h c) -> p c h", h=H),
                                        AX.X, ALU.add).then_inc(nsqd, 1)
                dve.wait_ge(remd, i + 1)
                nc.vector.tensor_copy(buffer(i)[:, 8:16], by_row(rem[:, i % 2])).then_inc(mid, 1)
                if c == "k":
                    dve.wait_ge(nsqd, i + 1)
                    nc.vector.tensor_reduce(kmax[0:PR, t:t + 1], ksq[:], AX.X, ALU.max).then_inc(maxd, 1)
                    if t == T - 1:
                        dve.wait_ge(maxd, T + 1)
                        nc.vector.tensor_reduce(kall[:, 0:1], kmax[:], AX.X, ALU.max).then_inc(maxd, 1)
            dve.wait_ge(rooted, 1)
            nc.vector.tensor_scalar(bound, bound, -1.0, -ADJ_GAIN, ALU.mult, ALU.add).then_inc(guard_steps, 1)
            dve.wait_ge(guard_steps, 1)
            dve.wait_ge(low, len(jobs))
            nc.vector.tensor_copy(guard[:, 0], bound).then_inc(guard_steps, 1)
            dve.wait_ge(guard_steps, 2)
            nc.vector.tensor_tensor(guard[:, 1], bound, guard[:, 0], ALU.subtract).then_inc(guard_steps, 1)

        @block.gpsimd
        def _(pool):
            for i, (c, t) in enumerate(jobs):
                pool.wait_ge(mid, i + 1)
                nc.gpsimd.tensor_tensor(buffer(i)[:, 16:24], by_row(rem[:, i % 2]), buffer(i)[:, 8:16],
                                        ALU.subtract).then_inc(low, 1)
                if i == T + 1:
                    pool.wait_ge(maxd, T + 2)
                    nc.gpsimd.partition_all_reduce(kall[:, 1:2], kall[:, 0:1], 128, bass.bass_isa.ReduceOp.max).then_inc(allmax, 1)


class Always:

    def __enter__(self):
        return self

    def __exit__(self, *_):
        return False


def when(eng, flag):
    if flag is None:
        return Always()
    return eng.If(eng.value_load(flag[0:1, 0:1], min_val=0, max_val=1) != 0)


def weigh(nc, keep):
    adj_b = keep["adj_b"].rearrange("p h a n -> p (h a) n")
    weight = keep["weight"][:].rearrange("p h a n -> p (h a) n")
    n = 2 * PAIRS
    with ExitStack() as ctx:
        last_row = ctx.enter_context(nc.sbuf_tensor("last_row", [PR, 2 * CH], BF16))
        done = ctx.enter_context(nc.semaphore("weights_done"))
        block = ctx.enter_context(nc.Block())

        @block.scalar
        def _(act):
            nc.scalar.copy(last_row[0:FULL], adj_b[0:FULL, n - 1]).then_inc(done, 1)
            act.wait_ge(done, 1)
            steps, lo = 1, 0
            while lo < n - 1:
                hi = min((n + lo) // 2, n - 1)
                cuts = sorted({lo, hi} | {c for c in (1, PAIRS, PAIRS + 1) if lo < c < hi})
                for c0, c1 in zip(cuts, cuts[1:]):
                    r = PR if c0 % PAIRS == 0 else FULL
                    nc.scalar.activation(weight[0:r, c0:c1], adj_b[0:r, c0:c1], ACT.Exp, scale=ADJ_GAIN).then_inc(done, 1)
                    steps += 1
                    act.wait_ge(done, steps)
                lo = hi
            nc.scalar.activation(weight[0:FULL, n - 1], last_row[0:FULL], ACT.Exp, scale=ADJ_GAIN).then_inc(done, 1)
            act.wait_ge(done, steps + 1)


def attend(nc, dram, keep, tag, flag=None):
    adj_a, weight = keep["adj_a"], keep["weight"]
    with ExitStack() as ctx:
        def sb(name, shape, dt=F32):
            return ctx.enter_context(nc.sbuf_tensor(name + tag, shape, dt))

        def sem(name):
            return ctx.enter_context(nc.semaphore(name + tag))

        prob = sb("prob", [PR, 3, NP])
        stacked = sb("stacked", [128, NP + 2 * N], BF16)
        q_st = stacked[:, 0:NP].rearrange("p (a n) -> p a n", a=2)
        k_st = stacked[:, NP:].rearrange("p (a n) -> p a n", a=2)
        v_in_sb = sb("v_in_sb", [PR, 2, T * H])
        v_aug = sb("v_aug", [PR, 2, T, H + 1])
        o_sb = sb("o_sb", [128, QT])
        S = ctx.enter_context(nc.psum_tensor("scores" + tag, [128, 6, 512], F32))
        O = ctx.enter_context(nc.psum_tensor("sums" + tag, [128, 2, 512], F32))

        ready = sem("ready")
        filled = sem("filled")
        q_in = [sem(f"q_in{j}") for j in range(2)]
        k_in = [sem(f"k_in{j}") for j in range(2)]
        v_in = [sem(f"v_in{j}") for j in range(2)]
        qk = sem("qk")
        added = sem("added")
        exps = sem("exps")
        pv = sem("pv")
        weighed = sem("weighed")
        v_placed = sem("v_placed")
        o_copied = sem("o_copied")
        stores = sem("stores")
        o_out = [sem(f"o_out{j}") for j in range(2)]
        QK0 = 2 * QK_HALF + 1
        PV0 = 2 * T - 4 + 1
        EXPS0 = 3
        block = ctx.enter_context(nc.Block())

        def buffer(s):
            return s % (2 * STEPS) % 3

        def back(s):
            return 2 if s < 2 * STEPS % 3 else 3

        def halves_multiplied(eng, n):
            eng.wait_ge(qk, n * QK_HALF + 1)

        def halves_summed(eng, n):
            eng.wait_ge(pv, n * T + 1)

        qd = dram["qd"]
        kd = dram["kd"]
        vflat = dram["vd"].rearrange("i c -> (i c)")

        @block.sync
        def _(sp):
            with when(sp, flag):
                def load_k(at, par):
                    for r0, n in ((0, 24), (24, 16), (40, 8)):
                        sp.dma_start(k_st[r0:r0 + n, par], kd[0:n, bass.ds(at, N)]).then_inc(k_in[par], 16)

                def load_q(at, half):
                    w = min(HALF, N - half * HALF)
                    cols = bass.ds(at, w)
                    for j in range(3):
                        sp.dma_start(q_st[8 * j:8 * j + 8, half, 0:w], qd[0:8, cols]).then_inc(q_in[half], 16)
                    for j in range(2):
                        sp.dma_start(q_st[24 + 8 * j:32 + 8 * j, half, 0:w], qd[8:16, cols]).then_inc(q_in[half], 16)
                    sp.dma_start(q_st[40:ROWS, half, 0:w], qd[16:26, cols]).then_inc(q_in[half], 16)

                def load_v(at, rest, par):
                    sp.dma_start(v_in_sb[0:FULL, par], vflat[bass.ds(at, FULL * T * H)].rearrange("(p c) -> p c", c=T * H))\
                      .then_inc(v_in[par], 16)
                    sp.dma_start(v_in_sb[FULL:PR, par, 0:REST * H],
                                 vflat[bass.ds(rest, REST * H)].rearrange("(p c) -> p c", p=1)).then_inc(v_in[par], 16)

                def store(at, half):
                    for j in range(4):
                        w = min(QT, N - half * HALF - j * QT)
                        sp.dma_start(dram["od"][0:H + 1, bass.ds(at[j], w)],
                                     o_sb[32 * j:32 * j + H + 1, 0:w]).then_inc(o_out[half], 16)

                sp.wait_ge(ready, 2)
                sp.wait_ge(filled, 1)
                with sp.Fori(0, HEADS // 2) as i:
                    for par in range(2):
                        at = i * (2 * N) + par * N
                        halves_multiplied(sp, i * 4 + 2 * par)
                        load_k(at, par)
                        sp.wait_ge(v_placed, i * 2 + par + 1)
                        load_v(at * H, at * H + FULL * T * H, par)
                        halves_multiplied(sp, i * 4 + 2 * par + 1)
                        load_q(at, 0)
                        sp.wait_ge(o_copied, i * 4 + 2 * par + 1)
                        sp.sem_inc(stores, 1)
                        store([at + j * QT for j in range(4)], 0)
                        halves_multiplied(sp, i * 4 + 2 * par + 2)
                        load_q(at + HALF, 1)
                        sp.wait_ge(o_copied, i * 4 + 2 * par + 2)
                        sp.sem_inc(stores, 1)
                        store([at + (HALF + j * QT) for j in range(4)], 1)
                sp.wait_ge(o_copied, 2 * HEADS + 1)
                store([HEADS * N + j * QT for j in range(4)], 0)
                sp.wait_ge(o_copied, 2 * HEADS + 2)
                store([HEADS * N + HALF + j * QT for j in range(4)], 1)
                for half in range(2):
                    sp.wait_ge(o_out[half], 64 * (HEADS + 1))

        @block.gpsimd
        def _(pool):
            with when(pool, flag):
                nc.gpsimd.memset(v_in_sb[:], 0.0)
                nc.gpsimd.memset(k_st, 1.0).then_inc(filled, 1)
                pool.wait_ge(filled, 1)
                pool.wait_ge(ready, 2)
                pool.sem_inc(v_placed, 2)
                pool.sem_inc(weighed, 2)
                with pool.Fori(0, HEADS // 2) as i:
                    for s in range(2 * STEPS):
                        par, half, pair = s // STEPS, s % STEPS // PAIRS, s % PAIRS
                        if s % STEPS == 0:
                            pool.wait_ge(v_in[par], i * 32 + 32)
                            halves_summed(pool, i * 4 + 2 * par)
                            v = v_in_sb[:, par].rearrange("p (t h) -> p t h", h=H)
                            nc.gpsimd.tensor_tensor(v_aug[:, par, :, 0:H], v, v_aug[:, par, :, H:H + 1].broadcast_to((PR, T, H)),
                                                    ALU.mult).then_inc(v_placed, 1)
                        r = rows(2 * pair)
                        p = prob[0:r, buffer(s), 4 * CH:6 * CH]
                        pool.wait_ge(exps, i * (4 * STEPS) + EXPS0 + 2 * s + 1)
                        nc.gpsimd.tensor_tensor(p, p, weight[0:r, half, pair], ALU.mult).then_inc(weighed, 1)

        @block.vector
        def _(dve):
            with when(dve, flag):
                nc.vector.memset(prob[:, 0:2], 0.0)
                nc.vector.memset(o_sb[:], 0.0)
                nc.vector.memset(O[:], 0.0)
                nc.vector.memset(q_st, 0.0)
                nc.vector.memset(v_aug[:], 0.0).then_inc(ready, 1)
                dve.wait_ge(ready, 1)
                nc.vector.memset(v_aug[0:FULL, :, REST:T, H:H + 1], 1.0)
                nc.vector.memset(v_aug[0:PR, :, 0:REST, H:H + 1], 1.0).then_inc(ready, 1)
                dve.wait_ge(ready, 2)
                dve.sem_inc(added, 2)
                dve.sem_inc(o_copied, 1)

                def copy_sums(n_full, n_out, half):
                    halves_summed(dve, n_full)
                    dve.wait_ge(o_out[1 - half], n_out)
                    nc.vector.tensor_copy(o_sb[:], O[:, half, 0:QT]).then_inc(o_copied, 1)

                with dve.Fori(0, HEADS // 2) as i:
                    for s in range(2 * STEPS):
                        par, half, pair = s // STEPS, s % STEPS // PAIRS, s % PAIRS
                        r = rows(2 * pair)
                        for u in BY_DVE:
                            dve.wait_ge(pv, i * (4 * STEPS) + PV0 + 2 * (s - back(s) + 2) + u + 1)
                            dve.wait_ge(qk, i * (6 * STEPS) + QK0 + 3 * s + u + 1)
                            cols = slice(2 * u * CH, 2 * (u + 1) * CH)
                            nc.vector.scalar_tensor_tensor(
                                out=prob[0:r, buffer(s), cols].rearrange("p (a b) -> p a b", b=CH),
                                in0=adj_a[0:r, half, pair, cols].rearrange("p (a b) -> p a b", b=CH), scalar=ADJ_GAIN,
                                in1=S[0:r, 2 * u:2 * u + 2, 0:CH], op0=ALU.mult, op1=ALU.add).then_inc(added, 1)
                        if pair == 1:
                            if half == 0:
                                copy_sums(i * 4 + 2 * par + 2, i * 128 + 64 * par + 64, 1)
                            else:
                                copy_sums(i * 4 + 2 * par + 3, i * 128 + 64 * par + 64, 0)
                copy_sums(2 * HEADS + 2, 64 * (HEADS + 1), 1)

        @block.scalar
        def _(act):
            with when(act, flag):
                act.wait_ge(ready, 2)
                act.sem_inc(exps, EXPS0)
                with act.Fori(0, HEADS // 2) as i:
                    for s in range(2 * STEPS):
                        r = rows(2 * (s % PAIRS))
                        act.wait_ge(qk, i * (6 * STEPS) + QK0 + 3 * s + 3)
                        if back(s) == 2:
                            act.wait_ge(pv, i * (4 * STEPS) + PV0 + 2 * s + 2)
                        nc.scalar.activation(prob[0:r, buffer(s), 4 * CH:6 * CH].rearrange("p (a b) -> p a b", b=CH),
                                             S[0:r, 4:6, 0:CH], ACT.Exp).then_inc(exps, 1)
                        p = prob[0:r, buffer(s), 0:4 * CH]
                        act.wait_ge(added, i * (4 * STEPS) + 2 * s + 4)
                        nc.scalar.activation(p, p, ACT.Exp).then_inc(exps, 1)

        @block.tensor
        def _(pe):
            with when(pe, flag):
                pe.wait_ge(ready, 2)
                pe.sem_inc(qk, QK0)
                pe.sem_inc(pv, PV0)

                def scores(i, s, u):
                    par, half, pair = s // STEPS, s % STEPS // PAIRS, s % PAIRS
                    if pair == 0 and u == 0:
                        pe.wait_ge(q_in[half], i * 192 + 96 * (par + 1))
                        if half == 0:
                            pe.wait_ge(k_in[par], i * 48 + 48)
                    if u in BY_DVE:
                        pe.wait_ge(added, i * (4 * STEPS) + 2 * s + u + 1)
                    else:
                        pe.wait_ge(exps, i * (4 * STEPS) + EXPS0 + 2 * s - 1)
                    for c in (2 * u, 2 * u + 1):
                        t, cols = 2 * pair + c // 3, slice(c % 3 * CH, (c % 3 + 1) * CH)
                        r = rows(t)
                        last = nc.tensor.matmul(S[0:r, c, 0:CH], k_st[:, par, t:t + T * (r - 1) + 1:T],
                                                q_st[:, half, cols], start=True, stop=True)
                    last.then_inc(qk, 1)

                def sums(i, s, j):
                    par, half, pair = s % (2 * STEPS) // STEPS, s % STEPS // PAIRS, s % PAIRS
                    t = 2 * pair + j
                    if j == 0:
                        pe.wait_ge(exps, i * (4 * STEPS) + EXPS0 + 2 * s + 2)
                    else:
                        pe.wait_ge(weighed, i * (2 * STEPS) + s + 3)
                    if t == 0:
                        pe.wait_ge(o_copied, i * 4 + 2 * par + 1 + half)
                        if half == 0:
                            pe.wait_ge(v_placed, i * 2 + par + 3)
                    r = rows(t)
                    for g in range(4):
                        last = nc.tensor.matmul(O[32 * g:32 * g + H + 1, half, 0:QT], v_aug[0:r, par, t, :],
                                                prob[0:r, buffer(s), j * HALF + g * QT:j * HALF + (g + 1) * QT],
                                                start=(t == 0), stop=(t == T - 1))
                    last.then_inc(pv, 1)

                for g in range(4):
                    nc.tensor.matmul(O[32 * g:32 * g + H + 1, 1, 0:QT], v_aug[0:FULL, 1, 0, :], prob[0:FULL, 1, 0:QT],
                                     start=True, stop=False)
                with pe.Fori(0, HEADS // 2) as i:
                    for s in range(2 * STEPS):
                        scores(i, s, 0)
                        sums(i, s - 2, 0)
                        scores(i, s, 1)
                        scores(i, s, 2)
                        sums(i, s - 2, 1)
                for s in (-2, -1):
                    for j in range(2):
                        sums(HEADS // 2, s, j)


def check_sums(nc, dram, flag):
    with ExitStack() as ctx:
        def sb(name, shape, dt=F32):
            return ctx.enter_context(nc.sbuf_tensor(name, shape, dt))

        def sem(name):
            return ctx.enter_context(nc.semaphore(name))

        den = sb("den", [128, N])
        fit = sb("fit", [128, N])
        worst = sb("worst", [128, 2])
        den_in = sem("den_in")
        step = sem("step_c")
        spread = sem("spread")
        block = ctx.enter_context(nc.Block())

        @block.sync
        def _(sp):
            sp.dma_start(den[:], dram["od"][H, N:N + G].rearrange("(p c) -> p c", c=N)).then_inc(den_in, 16)

        @block.vector
        def _(dve):
            dve.wait_ge(den_in, 16)
            nc.vector.tensor_scalar(fit[:], den[:], LEAST, 1e30, ALU.max, ALU.min).then_inc(step, 1)
            dve.wait_ge(step, 1)
            nc.vector.tensor_tensor(fit[:], fit[:], den[:], ALU.not_equal).then_inc(step, 1)
            dve.wait_ge(step, 2)
            nc.vector.tensor_reduce(worst[:, 0:1], fit[:], AX.X, ALU.max).then_inc(step, 1)
            dve.wait_ge(spread, 1)
            nc.vector.tensor_copy(flag[:], worst[:, 1:2]).then_inc(step, 1)
            dve.wait_ge(step, 4)

        @block.gpsimd
        def _(pool):
            pool.wait_ge(step, 3)
            nc.gpsimd.partition_all_reduce(worst[:, 1:2], worst[:, 0:1], 128, bass.bass_isa.ReduceOp.max).then_inc(spread, 1)


def true_guards(nc, dram, keep, flag):
    ident = keep["ident"]
    with ExitStack() as ctx:
        def sb(name, shape, dt=F32):
            return ctx.enter_context(nc.sbuf_tensor(name, shape, dt))

        def sem(name):
            return ctx.enter_context(nc.semaphore(name))

        q_st = sb("q_max", [TERMS, 128 * NB], BF16)
        k_st = sb("k_max", [TERMS, N], BF16)
        two = sb("two", [128, NB, 2])
        top = sb("top", [128, NB])
        guard = sb("guard", [NB, 2, 128], BF16)
        ps = ctx.enter_context(nc.psum_tensor("ps_max", [128, 8, 512], F32))
        qk_in = sem("qk_in")
        mult = sem("mult")
        reduced = sem("reduced")
        topped = sem("topped")
        turned = sem("turned_m")
        halved = sem("halved")
        stores = sem("stores_m")
        written = sem("written")
        block = ctx.enter_context(nc.Block())
        LAST = N - 5 * CH

        @block.sync
        def _(sp):
            with when(sp, flag):
                with sp.Fori(0, HEADS) as h:
                    at = h * N
                    cols = bass.ds(at, N)
                    qd, kd = dram["qd"], dram["kd"]
                    for r0, n in ((0, 24), (24, 16), (40, 8)):
                        sp.dma_start(k_st[r0:r0 + n], kd[0:n, cols]).then_inc(qk_in, 16)
                    for r0, p in ((0, 0), (8, 0), (16, 0), (24, 1), (32, 1), (40, 2)):
                        sp.dma_start(q_st[r0:r0 + 8, 0:N], qd[8 * p:8 * p + 8, cols]).then_inc(qk_in, 16)
                    whole = 128 * (NB - 1)
                    firsts = bass.ds(at, whole)
                    rest = bass.ds(at + whole, N - whole)
                    sp.wait_ge(halved, h * 2 + 2)
                    sp.sem_inc(stores, 1)
                    for j in range(2):
                        sp.dma_start(qd[24 + j, firsts].rearrange("(b c) -> b c", c=128), guard[0:NB - 1, j])\
                          .then_inc(written, 16)
                        sp.dma_start(qd[24 + j:25 + j, rest], guard[NB - 1:NB, j, 0:N - whole]).then_inc(written, 16)
                    sp.wait_ge(written, h * 64 + 64)
                    sp.sem_inc(stores, 1)

        @block.tensor
        def _(pe):
            with when(pe, flag):
                with pe.Fori(0, HEADS) as h:
                    pe.wait_ge(qk_in, h * 144 + 144)
                    pe.wait_ge(topped, h * 2 + 1)
                    for b in range(NB):
                        pe.wait_ge(reduced, h * NB + b + 1)
                        for c in range(6):
                            w = CH if c < 5 else LAST
                            last = nc.tensor.matmul(ps[:, c, 0:w], q_st[:, 128 * b:128 * (b + 1)],
                                                    k_st[:, c * CH:c * CH + w], start=True, stop=True)
                        last.then_inc(mult, 1)
                    pe.wait_ge(topped, h * 2 + 3)
                    nc.tensor.transpose(ps[0:NB, 6, 0:128], top[:], ident[:]).then_inc(turned, 1)

        @block.vector
        def _(dve):
            with when(dve, flag):
                nc.vector.memset(q_st[:, N:], 0.0).then_inc(topped, 1)
                dve.wait_ge(topped, 1)
                dve.sem_inc(reduced, 1)
                with dve.Fori(0, HEADS) as h:
                    for b in range(NB):
                        dve.wait_ge(mult, h * NB + b + 1)
                        nc.vector.tensor_reduce(two[:, b, 0:1], ps[:, 0:5, 0:CH], AX.XY, ALU.max)
                        nc.vector.tensor_reduce(two[:, b, 1:2], ps[:, 5, 0:LAST], AX.X, ALU.max).then_inc(reduced, 1)
                    dve.wait_ge(reduced, h * NB + NB + 1)
                    nc.vector.tensor_reduce(top[:], two[:], AX.X, ALU.max).then_inc(topped, 1)
                    dve.wait_ge(topped, h * 2 + 2)
                    nc.vector.tensor_scalar(top[:], top[:], -1.0, -ADJ_GAIN, ALU.mult, ALU.add).then_inc(topped, 1)
                    dve.wait_ge(turned, h + 1)
                    nc.vector.tensor_copy(guard[:, 0], ps[0:NB, 6, 0:128]).then_inc(halved, 1)
                    dve.wait_ge(halved, h * 2 + 1)
                    nc.vector.tensor_tensor(guard[:, 1], ps[0:NB, 6, 0:128], guard[:, 0], ALU.subtract).then_inc(halved, 1)


def finish(nc, dram, keep):
    ident = keep["ident"]
    RING = 3
    NORMS = ((0, 16), (16, T))
    with ExitStack() as ctx:
        def sb(name, shape, dt=F32):
            return ctx.enter_context(nc.sbuf_tensor(name, shape, dt))

        def sem(name):
            return ctx.enter_context(nc.semaphore(name))

        wo = sb("wo", [D, H, D])
        z = sb("z", [PR, RING, H + 1, 2 * D])
        res = sb("res", [PR, T, D])
        zT = sb("zT", [128, 2, H * 128])
        st = sb("st", [PR, T, 6])
        mv = sb("mv_f", [PR, T, 2])
        rs = sb("rs", [PR, T])
        ps = ctx.enter_context(nc.psum_tensor("ps2", [128, 8, 512], F32))
        w_in = sem("wo_in")
        y_in = sem("y_in")
        z_in = [sem(f"z_in{j}") for j in range(RING)]
        divided = sem("divided")
        turned = sem("turned_f")
        placed = sem("placed_f")
        out_mm = sem("out_mm")
        added = sem("added_f")
        varred = sem("varred_f")
        rooted = sem("rooted_f")
        normed = sem("normed_f")
        out_done = sem("out_done")
        chain = sem("chain_f")
        block = ctx.enter_context(nc.Block())

        def whole(a):
            return a[0:FULL * T].rearrange("(p t) d -> p t d", t=T)

        @block.sync
        def _(sp):
            def load(j):
                od, s = dram["od"][:, N:N + G], z_in[j % RING]
                sp.dma_start(z[0:FULL, j % RING],
                             od[:, 0:FULL * T * D].rearrange("r (p n) -> p r n", p=FULL)[:, :, 2 * j * D:2 * (j + 1) * D])\
                  .then_inc(s, 16)
                if j == 0:
                    sp.dma_start(z[FULL:PR, 0], od[:, FULL * T * D:G].rearrange("r (p n) -> p r n", p=1)).then_inc(s, 16)

            load(0)
            sp.dma_start(wo[:], dram["wo"]).then_inc(w_in, 16)
            load(1)
            sp.dma_start(res[0:FULL], whole(dram["y1"])).then_inc(y_in, 16)
            sp.dma_start(res[FULL:PR, 0:REST], dram["y1"][FULL * T:N].rearrange("(p t) d -> p t d", t=REST)).then_inc(y_in, 16)
            for j in range(2, PAIRS):
                if j >= RING:
                    sp.wait_ge(turned, 2 * (j - RING) + 2)
                load(j)
            for t0, t1 in NORMS:
                sp.wait_ge(normed, t1)
                sp.dma_start(whole(dram["out"])[:, t0:t1], res[0:FULL, t0:t1]).then_inc(out_done, 16)
                if t0 == 0:
                    sp.dma_start(dram["out"][FULL * T:N].rearrange("(p t) d -> p t d", t=REST), res[FULL:PR, 0:REST])\
                      .then_inc(out_done, 16)
            sp.wait_ge(out_done, 16 * (len(NORMS) + 1))

        @block.tensor
        def _(pe):
            def turn(t):
                n = rows(t)
                pe.wait_ge(divided, t // 2 + 1)
                if t >= 2:
                    pe.wait_ge(placed, t - 1)
                for h in range(H):
                    last = nc.tensor.transpose(ps[:, 2 * (t % 2) + h // 4, (h % 4) * 128:(h % 4) * 128 + n],
                                               z[0:n, (t // 2) % RING, h, (t % 2) * D:(t % 2 + 1) * D], ident[0:n, 0:n])
                last.then_inc(turned, 1)

            def out(t):
                n = rows(t)
                pe.wait_ge(placed, t + 1)
                if t >= 2:
                    pe.wait_ge(added, t - 1)
                for h in range(H):
                    last = nc.tensor.matmul(ps[0:n, 4 + t % 2, 0:D], zT[:, t % 2, h * 128:h * 128 + n], wo[:, h, :],
                                            start=(h == 0), stop=(h == H - 1))
                last.then_inc(out_mm, 1)

            pe.wait_ge(w_in, 16)
            turn(0)
            for t in range(1, T):
                turn(t)
                out(t - 1)
            out(T - 1)

        @block.scalar
        def _(act):
            for t in range(T):
                n = rows(t)
                act.wait_ge(turned, t + 1)
                if t >= 2:
                    act.wait_ge(out_mm, t - 1)
                nc.scalar.copy(zT[:, t % 2].rearrange("p (a h n) -> p a h n", a=2, n=128)[:, :, :, 0:n],
                               ps[:, 2 * (t % 2):2 * (t % 2) + 2, :].rearrange("p a (h n) -> p a h n", n=128)[:, :, :, 0:n])\
                  .then_inc(placed, 1)
            for i, (t0, t1) in enumerate(NORMS):
                act.wait_ge(varred, i + 1)
                nc.scalar.activation(rs[:, t0:t1], rs[:, t0:t1], ACT.Sqrt).then_inc(rooted, 1)

        @block.vector
        def _(dve):
            links = [0]

            def link(ins):
                links[0] += 1
                ins.then_inc(chain, 1)
                dve.wait_ge(chain, links[0])

            def divide(j):
                n, b = rows(2 * j), j % RING
                dve.wait_ge(z_in[b], 16 * (j // RING + (2 if b == 0 else 1)))
                link(nc.vector.reciprocal(z[0:n, b, H], z[0:n, b, H]))
                nc.vector.tensor_tensor(z[0:n, b, 0:H], z[0:n, b, 0:H],
                                        z[0:n, b, H:H + 1].broadcast_to((n, H, 2 * D)), ALU.mult).then_inc(divided, 1)

            def add(t):
                n = rows(t)
                dve.wait_ge(out_mm, t + 1)
                nc.vector.tensor_tensor(res[0:n, t], ps[0:n, 4 + t % 2, 0:D], res[0:n, t], ALU.add).then_inc(added, 1)

            def normalise(i):
                t0, t1 = NORMS[i]
                dve.wait_ge(added, t1)
                for t in range(t0, t1):
                    last = nc.vector.bn_stats(st[0:rows(t), t], res[0:rows(t), t])
                link(last)
                for t in range(t0, t1):
                    last = nc.vector.bn_aggr(mv[0:rows(t), t], st[0:rows(t), t])
                link(last)
                nc.vector.tensor_scalar(rs[:, t0:t1], mv[:, t0:t1, 1], EPS, None, ALU.add).then_inc(varred, 1)
                dve.wait_ge(rooted, i + 1)
                link(nc.vector.reciprocal(rs[:, t0:t1], rs[:, t0:t1]))
                for t in range(t0, t1):
                    n = rows(t)
                    nc.vector.tensor_scalar(res[0:n, t], res[0:n, t], mv[0:n, t, 0:1], rs[0:n, t:t + 1],
                                            ALU.subtract, ALU.mult).then_inc(normed, 1)

            link(nc.vector.memset(mv[:], 0.0))
            divide(0)
            divide(1)
            dve.wait_ge(y_in, 32)
            for t in range(T):
                if t % 2 == 0 and t // 2 + 2 < PAIRS:
                    divide(t // 2 + 2)
                add(t)
                for i, (t0, t1) in enumerate(NORMS):
                    if t == min(t1 + 1, T - 1):
                        normalise(i)


def adj_attention_kernel(nc, x, adjT, W, b, wq, wk, wv, wo, out):
    def scratch(name, shape, dt=F32):
        return nc.dram_tensor(name, shape, dt, kind="Internal").ap()

    dram = {"x": x, "adjT": adjT, "W": W, "b": b, "wq": wq, "wk": wk, "wv": wv, "wo": wo, "out": out,
            "y1": scratch("y1_d", [N, D]), "qd": scratch("q_d", [26, G], BF16), "kd": scratch("k_d", [24, G], BF16),
            "vd": scratch("v_d", [N, CW]), "od": scratch("o_d", [H + 1, N + G])}
    with ExitStack() as ctx:
        weight = ctx.enter_context(nc.sbuf_tensor("weight", [128, 2, PAIRS, 2 * CH], F32))
        flat = weight[:].rearrange("p h a n -> p (h a n)")
        half = 2 * PAIRS * CH
        keep = {"adj_a": ctx.enter_context(nc.sbuf_tensor("adj_a", [PR, 2, PAIRS, 4 * CH], BF16)),
                "ident": ctx.enter_context(nc.sbuf_tensor("ident", [128, 128], F32)),
                "weight": weight,
                "spare": flat[:, 0:half],
                "adj_b": flat[0:PR, half:].bitcast(BF16).rearrange("p (h a n) -> p h a n", h=2, a=PAIRS)}
        with nc.sbuf_tensor("yT", [D, T * PR], F32) as yT:
            keep["yT"] = yT
            layer0(nc, dram, keep)
            project(nc, dram, keep)
        weigh(nc, keep)
        attend(nc, dram, keep, "")
        with nc.sbuf_tensor("flag", [128, 1], I32) as flag:
            check_sums(nc, dram, flag)
            true_guards(nc, dram, keep, flag)
            attend(nc, dram, keep, "_again", flag)
        finish(nc, dram, keep)


def kernel(**inputs):
    import numpy as _np
    import concourse.bacc as _bacc
    from concourse import mybir as _mybir
    from concourse.bass_utils import run_bass_kernel_spmd as _run

    def turned(name):
        return _np.ascontiguousarray(_np.asarray(inputs[name]).T)

    def by_column(name):
        w = _np.asarray(inputs[name])
        return _np.ascontiguousarray(w.reshape(D, H, D).transpose(2, 1, 0)).reshape(D, CW)

    given = {
        "x": _np.ascontiguousarray(inputs["x"]), "adjT": turned("adj"),
        "W": _np.ascontiguousarray(inputs["L0_gnn_W"]), "b": _np.ascontiguousarray(inputs["L0_gnn_b"]),
        "wq": by_column("L1_gnn_Wq"), "wk": by_column("L1_gnn_Wk"), "wv": turned("L1_gnn_Wv"),
        "wo": turned("L1_gnn_Wo").reshape(D, H, D),
    }
    nc = _bacc.Bacc("TRN2", target_bir_lowering=False, num_devices=1)
    arrays, args = {}, []
    for name, a in given.items():
        arrays[f"in_{name}_dram"] = a
        args.append(nc.dram_tensor(f"in_{name}_dram", a.shape, _mybir.dt.from_np(a.dtype), kind="ExternalInput").ap())
    args.append(nc.dram_tensor("out_0_dram", (N, D), _mybir.dt.float32, kind="ExternalOutput").ap())
    adj_attention_kernel(nc, *args)
    r = _run(nc, [arrays], core_ids=[0])
    return r.results[0]["out_0_dram"]
```
